# Optimizing a Trainium2 kernel written in Bass

```python
import numpy as np
import jax
import jax.numpy as jnp

def _softmax(x, axis=-1):
    return jax.nn.softmax(x, axis=axis)

def _gelu(x):
    return jax.nn.gelu(x, approximate=True)

def _silu(x):
    return jax.nn.silu(x)

def _sigmoid(x):
    return jax.nn.sigmoid(x)

def _layernorm(x, axis=-1, eps=1e-05):
    m = jnp.mean(x, axis=axis, keepdims=True)
    v = jnp.var(x, axis=axis, keepdims=True)
    return (x - m) / jnp.sqrt(v + eps)

def _scatter_add(tgt, idx, src, axis=0):
    return tgt.at[idx].add(src)

def _segment_sum(src, seg, n):
    return jax.ops.segment_sum(src, seg, n)
kernel_name = 'mk_flamingo_gated_d1_seqx_r8_89dc6f'

def setup_inputs(seed: int=0):
    np.random.seed(seed)
    _w = jnp.asarray

    def _rec_inputs():
        import jax
        import jax.numpy as jnp
        _rk = jax.random.key(seed)
        x = -0.0003929 + 0.9999 * jax.random.normal(jax.random.fold_in(_rk, 1), (8, 100, 256), jnp.float32)
        _lenS = 100 - jax.random.randint(jax.random.fold_in(_rk, 7), (8,), 0, max(1, 100 // 4) + 1, jnp.int32)
        _lenS2 = 1444 - jax.random.randint(jax.random.fold_in(_rk, 8), (8,), 0, max(1, 1444 // 4) + 1, jnp.int32)
        _ctx_2048P = jax.random.normal(jax.random.fold_in(_rk, 11), (8, 16, 256), jnp.float32)
        _ctx_2048c = jax.random.dirichlet(jax.random.fold_in(_rk, 511), 0.3 * jnp.ones((16,), jnp.float32), (8, 1444))
        _ctx_2048t = jnp.einsum('bsk,bkd->bsd', _ctx_2048c, _ctx_2048P)
        _ctx_2048t = _ctx_2048t * jax.lax.rsqrt(jnp.mean(jnp.square(_ctx_2048t)) + 1e-12) * 0.953939
        ctx_2048 = 2.81802e-05 + 1.00001 * (_ctx_2048t + 0.3 * jax.random.normal(jax.random.fold_in(_rk, 611), (8, 1444, 256), jnp.float32))
        _g = jax.random.normal(jax.random.fold_in(_rk, 9001), (2, 1), jnp.float32)
        _g = jnp.sign(_g) * jnp.maximum(jnp.abs(_g), 1.0) + (_g == 0) * 1.0
        g_xattn = _g[0]
        g_ffn = _g[1]
        return (x, ctx_2048, g_xattn, g_ffn)
    x, ctx_2048, g_xattn, g_ffn = _rec_inputs()

    def _L0_xattn_setup():
        import jax, jax.numpy as jnp
        import numpy as np
        B, S, D = (8, 128, 256)
        H, HD = (16, 128)
        key = jax.random.key(seed)
        ks = jax.random.split(key, 6)
        fan_in = 1.0 / np.sqrt(D)
        return {'inputs_q': jax.random.normal(ks[0], (B, S, D), jnp.float32), 'inputs_kv': jax.random.normal(ks[1], (B, S, D), jnp.float32), 'Wq': jax.random.normal(ks[2], (D, H * HD), jnp.float32) * fan_in, 'Wk': jax.random.normal(ks[3], (D, H * HD), jnp.float32) * fan_in, 'Wv': jax.random.normal(ks[4], (D, H * HD), jnp.float32) * fan_in, 'Wo': jax.random.normal(ks[5], (H * HD, D), jnp.float32) * (1.0 / np.sqrt(H * HD))}
    _L0_xattn_all = _L0_xattn_setup()
    _L0_xattn_in = {k: v for k, v in _L0_xattn_all.items() if k in ('Wq', 'Wk', 'Wv', 'Wo')}
    del _L0_xattn_all

    def _L0_ffn_setup():
        import jax, jax.numpy as jnp
        import numpy as np
        TOP_K = 6
        CAP_FACTOR = 2

        def _shared_swiglu(x, wg, wu, wd):
            return jax.nn.silu(x @ wg.T) * (x @ wu.T) @ wd.T
        key = jax.random.key(seed)
        ks = jax.random.split(key, 8)
        B, S, D, E, F, FS = (4, 256, 256, 64, 176, 352)
        scale = jnp.float32(0.02)
        return {'hidden_states': jax.random.normal(ks[0], (B, S, D), jnp.float32), 'gate_w': jax.random.normal(ks[1], (E, D), jnp.float32) * scale, 'w_gate': jax.random.normal(ks[2], (E, F, D), jnp.float32) * scale, 'w_up': jax.random.normal(ks[3], (E, F, D), jnp.float32) * scale, 'w_down': jax.random.normal(ks[4], (E, D, F), jnp.float32) * scale, 'sh_gate': jax.random.normal(ks[5], (FS, D), jnp.float32) * scale, 'sh_up': jax.random.normal(ks[6], (FS, D), jnp.float32) * scale, 'sh_down': jax.random.normal(ks[7], (D, FS), jnp.float32) * scale}
    _L0_ffn_all = _L0_ffn_setup()
    _L0_ffn_in = {k: v for k, v in _L0_ffn_all.items() if k in ('gate_w', 'w_gate', 'w_up', 'w_down', 'sh_gate', 'sh_up', 'sh_down')}
    del _L0_ffn_all
    return {'x': x, 'ctx_2048': ctx_2048, 'g_xattn': g_xattn, 'g_ffn': g_ffn, 'L0_xattn_Wq': _L0_xattn_in['Wq'], 'L0_xattn_Wk': _L0_xattn_in['Wk'], 'L0_xattn_Wv': _L0_xattn_in['Wv'], 'L0_xattn_Wo': _L0_xattn_in['Wo'], 'L0_ffn_gate_w': _L0_ffn_in['gate_w'], 'L0_ffn_w_gate': _L0_ffn_in['w_gate'], 'L0_ffn_w_up': _L0_ffn_in['w_up'], 'L0_ffn_w_down': _L0_ffn_in['w_down'], 'L0_ffn_sh_gate': _L0_ffn_in['sh_gate'], 'L0_ffn_sh_up': _L0_ffn_in['sh_up'], 'L0_ffn_sh_down': _L0_ffn_in['sh_down']}

def reference(x, ctx_2048, g_xattn, g_ffn, L0_xattn_Wq, L0_xattn_Wk, L0_xattn_Wv, L0_xattn_Wo, L0_ffn_gate_w, L0_ffn_w_gate, L0_ffn_w_up, L0_ffn_w_down, L0_ffn_sh_gate, L0_ffn_sh_up, L0_ffn_sh_down):
    import jax
    import jax.numpy as jnp

    def _L0_xattn_ref(inputs_q, inputs_kv, Wq, Wk, Wv, Wo):
        import jax, jax.numpy as jnp
        import numpy as np
        B, S, D = (8, 128, 256)
        H, HD = (16, 128)
        b, sq, _ = inputs_q.shape
        skv = inputs_kv.shape[1]
        q = (inputs_q @ Wq).reshape(b, sq, H, HD) * (1.0 / np.sqrt(HD))
        k = (inputs_kv @ Wk).reshape(b, skv, H, HD)
        v = (inputs_kv @ Wv).reshape(b, skv, H, HD)
        scores = jnp.einsum('bqhd,bkhd->bhqk', q, k)
        attn = jax.nn.softmax(scores, axis=-1)
        ctx = jnp.einsum('bhqk,bkhd->bqhd', attn, v).reshape(b, sq, H * HD)
        return ctx @ Wo

    def _L0_ffn_ref(hidden_states, gate_w, w_gate, w_up, w_down, sh_gate, sh_up, sh_down):
        import jax, jax.numpy as jnp
        import numpy as np
        TOP_K = 6
        CAP_FACTOR = 2

        def _shared_swiglu(x, wg, wu, wd):
            return jax.nn.silu(x @ wg.T) * (x @ wu.T) @ wd.T
        B, S, D = hidden_states.shape
        E = gate_w.shape[0]
        x = hidden_states.reshape(-1, D)
        N = x.shape[0]
        A = N * TOP_K
        C = CAP_FACTOR * ((A + E - 1) // E)
        scores = jax.nn.softmax(x @ gate_w.T, axis=-1)
        topk_w, topk_idx = jax.lax.top_k(scores, TOP_K)
        topk_w = topk_w / (topk_w.sum(-1, keepdims=True) + 1e-20)
        flat_e = topk_idx.reshape(-1)
        flat_w = topk_w.reshape(-1)
        order = jnp.argsort(flat_e)
        se = flat_e[order]
        st = order // TOP_K
        sw = flat_w[order]
        counts = jnp.bincount(flat_e, length=E)
        offsets = jnp.cumsum(counts) - counts
        pos = jnp.arange(A) - offsets[se]
        valid = pos < C
        pos_c = jnp.minimum(pos, C - 1)
        buf = jnp.zeros((E, C, D), x.dtype).at[se, pos_c].add(jnp.where(valid[:, None], x[st], jnp.zeros((), x.dtype)))
        g = jnp.einsum('ecd,efd->ecf', buf, w_gate)
        u = jnp.einsum('ecd,efd->ecf', buf, w_up)
        eo = jnp.einsum('ecf,edf->ecd', jax.nn.silu(g) * u, w_down)
        gathered = eo[se, pos_c] * (sw * valid.astype(sw.dtype))[:, None]
        y = jnp.zeros_like(x).at[st].add(gathered).reshape(B, S, D)
        return y + _shared_swiglu(hidden_states, sh_gate, sh_up, sh_down)
    x = x + jnp.tanh(g_xattn[0]) * _L0_xattn_ref(_layernorm(x, axis=-1), ctx_2048, L0_xattn_Wq, L0_xattn_Wk, L0_xattn_Wv, L0_xattn_Wo)
    x = x + jnp.tanh(g_ffn[0]) * _L0_ffn_ref(_layernorm(x, axis=-1), L0_ffn_gate_w, L0_ffn_w_gate, L0_ffn_w_up, L0_ffn_w_down, L0_ffn_sh_gate, L0_ffn_sh_up, L0_ffn_sh_down)
    return x

_drawn_inputs = setup_inputs


def setup_inputs(seed=0):
    import zlib

    import numpy as np

    out = dict(_drawn_inputs(seed))
    spreads = {}
    factors = {'L0_ffn_gate_w': 8.0,
     'L0_ffn_w_gate': 8.0,
     'L0_ffn_w_up': 8.0,
     'L0_ffn_w_down': 8.0,
     'L0_ffn_sh_gate': 3.274,
     'L0_ffn_sh_up': 3.278,
     'L0_ffn_sh_down': 3.265}
    for name, (base, spread) in spreads.items():
        noise = np.random.default_rng([zlib.crc32(name.encode()), seed]).standard_normal(out[name].shape)
        drawn = base * np.exp(spread * noise) if base else spread * noise
        out[name] = jnp.asarray(drawn.astype(out[name].dtype))
    for name, factor in factors.items():
        out[name] = (out[name] * factor).astype(out[name].dtype)
    return out
```

```python
from contextlib import ExitStack

import numpy as np
import concourse.bass as bass
from concourse import mybir

ALU = mybir.AluOpType
ACT = mybir.ActivationFunctionType
AX = mybir.AxisListType
F32 = mybir.dt.float32
F16 = mybir.dt.float16
BF16 = mybir.dt.bfloat16
U32 = mybir.dt.uint32

B, S, D = 8, 100, 256
H, HD = 16, 128
KV = 1444
DC = D // 128
KC = 12
KP = -(-KV // KC)
KLAST = KV - (KC - 1) * KP
KPAD = KC * KP
Q = H * S
TILES = -(-Q // 128)
TLAST = Q - (TILES - 1) * 128
PAIRS = B // 2
EPS = 1e-5
QSCALE = float(HD) ** -0.5
PSCALE = 16384.0
F16MAX = 65504.0

E, F, FS, TOPK = 64, 176, 352, 6
NTOK = B * S
CAP = 2 * -(-NTOK * TOPK // E)
SC = 2
SP_ = CAP // SC
FP = 88
FC = F // FP
FSC = FS // FP
DUMP = E * CAP

STEPS = 2 * TILES
GROUPS = [(0, 1), (2, 3), (4, 5), (6, 7), (8, 9), (10, 11, 12)]
NG = len(GROUPS)


def tile_rows(t):
    return TLAST if t % TILES == TILES - 1 else 128


def group_of(t):
    return min((t % TILES) // 2, NG - 1)


def group_width(g):
    return sum(tile_rows(t) for t in GROUPS[g])


Q_FIRST = {0: [(0, 0), (0, 1)]}
Q_AFTER = {0: [1, 2], 1: [3, 4], 2: [5, 6], 3: [7]}
QFILLS = H // 2 * DC
TBANKS = KC // 4


def fills_of_step(s):
    out = []
    if 1 <= s <= STEPS:
        out += [("T", s - 1, k) for k in range(TBANKS)]
    for hp in Q_AFTER.get(s, []):
        out += [("q", hp, c) for c in range(DC)]
    return out


FILL = {}
for _s in range(STEPS + 1):
    for _f in [("q", hp, c) for hp, c in Q_FIRST.get(_s, [])] + fills_of_step(_s):
        FILL[_f] = len(FILL)
FILLS = len(FILL)
assert FILLS % 2 == 0 and FILLS == QFILLS + TBANKS * STEPS

PV = {}
for _j in range(2):
    _o = _j * TILES
    for _g in range(4):
        PV[_o + 2 * _g + 3] = (_j, _g, 0, 6)
        PV[_o + 2 * _g + 4] = (_j, _g, 6, 12)
    for _n in range(3):
        PV[_o + 11 + _n] = (_j, 4, 4 * _n, 4 * _n + 4)
    PV[_o + 14] = (_j, 5, 0, 6)
    PV[_o + 15] = (_j, 5, 6, 12)
Y_STEP = {16: 0, 28: 1}
ALL_STEPS = STEPS + 3

XFILLS = PAIRS
SETUP_FILLS = XFILLS + 2 * H
QUADS = H // 4
PIECES = 10


def gated_cross_attention_moe(nc, x, ctx_rows, ctx_cols, wq_t, wk_t, wv_t, wo, g_xattn, g_ffn, gate_t,
                              eg_t, eu_t, ed_t, sg_t, su_t, sd_t, out):
    xn_rows = nc.dram_tensor("xn_rows", [DUMP + NTOK * TOPK, D], F32, kind="Internal").ap()
    eo_rows = nc.dram_tensor("eo_rows", [E * CAP, D], F32, kind="Internal").ap()
    attn_rows = nc.dram_tensor("attn_rows", [B, S, D], F32, kind="Internal").ap()

    stack = ExitStack()
    with stack:
        def sb(where, name, shape, dt=F32):
            return where.enter_context(nc.sbuf_tensor(name, shape, dt))

        def sem(name):
            return stack.enter_context(nc.semaphore(name))

        ps = stack.enter_context(nc.psum_tensor("ps", [128, 8, 512], F32))
        scores = ps[:, 0:3, :].rearrange("p a n -> p (a n)")
        stage = ps[:, 3:5, :]
        acc = ps[:, 5:7, :]
        yps = ps[:, 7, :]

        ident = sb(stack, "ident", [128, 128])
        gates = sb(stack, "gates", [128, 4])
        stats = sb(stack, "stats", [128, B, 6])
        mean_var = sb(stack, "mean_var", [128, B, 2])
        rstd = sb(stack, "rstd", [128, B])
        std = sb(stack, "std", [128, B])

        attn = ExitStack()
        xt_hi = sb(attn, "xt_hi", [128, DC, NTOK], F16)
        xt_lo = sb(attn, "xt_lo", [128, DC, NTOK], BF16)
        m_hi = sb(attn, "m_hi", [128, H, DC, D], F16)
        m_lo = sb(attn, "m_lo", [128, H, DC, D], BF16)
        n_hi = sb(attn, "n_hi", [128, H, DC, D], F16)
        n_lo = sb(attn, "n_lo", [128, H, DC, D], BF16)
        q_hi = sb(attn, "q_hi", [128, DC, 2, Q], F16)
        q_lo = sb(attn, "q_lo", [128, DC, 2, Q], BF16)
        ct_hi = sb(attn, "ct_hi", [128, 2, DC, KV], F16)
        ct_lo = sb(attn, "ct_lo", [128, 2, DC, KV], BF16)
        c_hi = sb(attn, "c_hi", [128, 2, KC, D], F16)
        c_lo = sb(attn, "c_lo", [128, 2, KC, D], BF16)
        raw = sb(attn, "raw", [128, 2, KV // 2])
        y_out = sb(attn, "y_out", [128, 2, D])
        neg_max = sb(attn, "neg_max", [128, 2])
        row_sum = sb(attn, "row_sum", [128, 2])
        row_inv = sb(attn, "row_inv", [128, 2])
        setup = ExitStack()
        x_in = sb(setup, "x_in", [128, B, D])
        x_norm = sb(setup, "x_norm", [128, B, D])
        w_raw = sb(setup, "w_raw", [128, 2, 2, 4, D])
        setup.close()
        probs = sb(attn, "probs", [128, 2, KPAD])
        pt_hi = [sb(attn, f"pt_hi{n}", [128, KC, group_width(4 + n)], F16) for n in range(2)]
        pt_lo = [sb(attn, f"pt_lo{n}", [128, KC, group_width(4 + n)], BF16) for n in range(2)]
        ut_hi = sb(attn, "ut_hi", [128, DC, Q], F16)
        ut_lo = sb(attn, "ut_lo", [128, DC, Q], BF16)
        attn.close()

        ffn = ExitStack()
        x1 = sb(ffn, "x1", [128, B, D])
        xn = sb(ffn, "xn", [128, B, D])
        xres = sb(ffn, "xres", [128, B, D])
        xnt = sb(ffn, "xnt", [128, DC, NTOK])
        gate_w = sb(ffn, "gate_w", [128, DC, E])
        ex = sb(ffn, "ex", [128, B, E])
        nmx = sb(ffn, "nmx", [128, B])
        esum = sb(ffn, "esum", [128, B])
        top = sb(ffn, "top", [128, B, 8])
        topi = sb(ffn, "topi", [128, B, 8], U32)
        topf = sb(ffn, "topf", [128, B, TOPK])
        wsum = sb(ffn, "wsum", [128, B])
        wk = sb(ffn, "wk", [128, B, TOPK])
        iota_e = sb(ffn, "iota_e", [128, E])
        dump_row = sb(ffn, "dump_row", [128, B, TOPK])
        hot = sb(ffn, "hot", [128, B, TOPK, E], BF16)
        hotpos = sb(ffn, "hotpos", [128, B, TOPK, E])
        mask = sb(ffn, "mask", [128, B, E], BF16)
        ones = sb(ffn, "ones", [128, S], BF16)
        tri = sb(ffn, "tri", [128, S], BF16)
        possb = sb(ffn, "possb", [128, B, E])
        pos = sb(ffn, "pos", [128, B, TOPK])
        over = sb(ffn, "over", [128, B, TOPK])
        slot = sb(ffn, "slot", [128, B, TOPK])
        scat = sb(ffn, "scat", [128, B, TOPK])
        slot_u = sb(ffn, "slot_u", [128, B * TOPK], U32)
        scat_u = sb(ffn, "scat_u", [128, B * TOPK], U32)
        shg = sb(ffn, "shg", [128, DC, FS])
        shu = sb(ffn, "shu", [128, DC, FS])
        shd = sb(ffn, "shd", [FP, FSC, D])
        sh_act = sb(ffn, "sh_act", [FP, 2, NTOK // 2])
        sh_h = sb(ffn, "sh_h", [FP, FSC, NTOK])
        sh_out = sb(ffn, "sh_out", [128, B, D])
        NW = 4
        wg = sb(ffn, "wg", [128, NW, DC, F])
        wu = sb(ffn, "wu", [128, NW, DC, F])
        wd = sb(ffn, "wd", [FP, NW, FC, D])
        xe = sb(ffn, "xe", [SP_, NW, SC, D])
        xet = sb(ffn, "xet", [128, 2, DC, CAP])
        act = sb(ffn, "act", [FP, 2, FC, CAP])
        hid = sb(ffn, "hid", [FP, 2, FC, CAP])
        eo = sb(ffn, "eo", [SP_, 2, SC, D])
        back = sb(ffn, "back", [128, 2, TOPK, D])
        ffn.close()
        zero = sb(stack, "zero", [1, 1])

        s_x, s_g, s_ident = sem("s_x"), sem("s_g"), sem("s_ident")
        s_dve, s_pool = sem("s_dve"), sem("s_pool")
        s_var, s_std, s_xnorm, s_tanh = sem("s_var"), sem("s_std"), sem("s_xnorm"), sem("s_tanh")
        s_w = [sem("s_w0"), sem("s_w1")]
        s_wused = sem("s_wused")
        s_full, s_hi, s_free = sem("s_full"), sem("s_hi"), sem("s_free")
        s_scores, s_max, s_exp, s_inv, s_norm = (sem(n) for n in ("s_scores", "s_max", "s_exp", "s_inv", "s_norm"))
        s_accfull, s_uhi, s_accfree = sem("s_accfull"), sem("s_uhi"), sem("s_accfree")
        s_yfull, s_yfree = sem("s_yfull"), sem("s_yfree")
        s_yst = [sem("s_yst0"), sem("s_yst1")]
        s_raw = [sem("s_raw0"), sem("s_raw1")]
        s_split = sem("s_split")
        s_pads, s_seen = sem("s_pads"), sem("s_seen")
        s_z, s_zero = sem("s_z"), sem("s_zero")
        s_res, s_att, s_fw = sem("s_res"), sem("s_att"), sem("s_fw")
        s_var2, s_std2, s_xn2 = sem("s_var2"), sem("s_std2"), sem("s_xn2")
        s_tfull, s_tdone = sem("s_tfull"), sem("s_tdone")
        s_logit, s_nmx, s_ex = sem("s_logit"), sem("s_nmx"), sem("s_ex")
        s_mask, s_posps, s_slot = sem("s_mask"), sem("s_posps"), sem("s_slot")
        s_scat, s_const = sem("s_scat"), sem("s_const")
        s_shup, s_shact, s_shh, s_shdown, s_shout = (sem(n) for n in ("s_shup", "s_shact", "s_shh", "s_shdown", "s_shout"))
        s_we = [sem(f"s_we{n}") for n in range(4)]
        s_xe = [sem(f"s_xe{n}") for n in range(4)]
        s_xt, s_xtc, s_up, s_act, s_hid, s_down, s_eo = (sem(n) for n in ("s_xt", "s_xtc", "s_up", "s_act", "s_hid", "s_down", "s_eo"))
        s_eost = [sem("s_eost0"), sem("s_eost1")]
        s_back = [sem("s_back0"), sem("s_back1")]
        s_comb, s_out, s_fin = sem("s_comb"), sem("s_out"), sem("s_fin")

        xr = x.rearrange("b s d -> s b d")
        heads4 = lambda w, n: w[bass.ds(n * 4 * HD, 4 * HD), :].rearrange("(h p) d -> p h d", p=HD)

        block = stack.enter_context(nc.Block())

        @block.sync
        def _(sp):
            for k in range(2):
                sp.sem_inc(s_yst[k], 16)
                sp.sem_inc(s_eost[k], 16)
            sp.dma_start(x_in[0:S, :, :], xr).then_inc(s_x, 16)
            sp.dma_start(gates[:, 0:1], g_xattn.partition_broadcast(128)).then_inc(s_g, 16)
            sp.dma_start(gates[:, 1:2], g_ffn.partition_broadcast(128)).then_inc(s_g, 16)

            def weights(pair, first, second, fresh):
                for k in range(2):
                    if not fresh:
                        sp.wait_ge(s_wused, pair * 2 + k - 1)
                    sp.dma_start(w_raw[:, k, 0], heads4(first, (pair * 2 + k) % QUADS)).then_inc(s_w[k], 16)
                    sp.dma_start(w_raw[:, k, 1], heads4(second, (pair * 2 + k) % QUADS)).then_inc(s_w[k], 16)

            def context(n, j, fresh):
                for k in range(PIECES):
                    if not (fresh and j == 0 and k < 2):
                        sp.wait_ge(s_split, n * PIECES + k - 1)
                    dst = raw[:, k % 2]
                    if k < 4:
                        c, half = k // 2, k % 2
                        sp.dma_start(dst, ctx_cols[bass.ds(n, 1), c * 128:(c + 1) * 128, half * (KV // 2):(half + 1) * (KV // 2)]
                                     .rearrange("o p n -> (o p) n")).then_inc(s_raw[k % 2], 16)
                    else:
                        c = 2 * (k - 4)
                        dst = dst[:, 0:2 * D].rearrange("p (c d) -> p c d", c=2)
                        src = ctx_rows[bass.ds(n, 1), :, :].rearrange("o n d -> (o n) d")
                        if c + 2 < KC:
                            sp.dma_start(dst[0:KP], src[c * KP:(c + 2) * KP, :].rearrange("(c p) d -> p c d", p=KP)).then_inc(s_raw[k % 2], 16)
                        else:
                            sp.dma_start(dst[0:KP, 0], src[c * KP:(c + 1) * KP, :]).then_inc(s_raw[k % 2], 16)
                            sp.dma_start(dst[0:KLAST, 1], src[(c + 1) * KP:KV, :]).then_inc(s_raw[k % 2], 16)

            weights(0, wq_t, wk_t, True)
            weights(1, wq_t, wk_t, False)
            context(0, 0, True)
            weights(2, wv_t, wo, False)
            weights(3, wv_t, wo, False)
            context(1, 1, True)
            sp.wait_ge(s_z, 1)
            sp.dma_start(xn_rows[0:DUMP, :].rearrange("(p r) d -> p r d", p=128),
                         y_out[:, 0:1, :].to_broadcast([128, DUMP // 128, D])).then_inc(s_zero, 16)
            with sp.Fori(1, PAIRS) as i:
                context(2 * i, 0, False)
                context(2 * i + 1, 1, False)

            sp.wait_ge(s_yst[0], 16 * (PAIRS + 1))
            sp.wait_ge(s_yst[1], 16 * (PAIRS + 1))
            sp.dma_start(x1[0:S], xr).then_inc(s_res, 16)
            sp.dma_start(xres[0:S], attn_rows.rearrange("b s d -> s b d")).then_inc(s_att, 16)
            sp.dma_start(gate_w[:], gate_t.rearrange("(c p) e -> p c e", p=128)).then_inc(s_fw, 16)
            sp.dma_start(shg[:], sg_t.rearrange("(c p) f -> p c f", p=128)).then_inc(s_fw, 16)
            sp.dma_start(shu[:], su_t.rearrange("(c p) f -> p c f", p=128)).then_inc(s_fw, 16)
            sp.dma_start(shd[:], sd_t.rearrange("(c p) d -> p c d", p=FP)).then_inc(s_fw, 16)

            def expert_weights(e, k, fresh):
                if not fresh:
                    sp.wait_ge(s_down, e - NW + 1)
                one = lambda w: w[bass.ds(e, 1)]
                sp.dma_start(wg[:, k], one(eg_t).rearrange("o p c f -> (o p) c f")).then_inc(s_we[k], 16)
                sp.dma_start(wu[:, k], one(eu_t).rearrange("o p c f -> (o p) c f")).then_inc(s_we[k], 16)
                sp.dma_start(wd[:, k], one(ed_t).rearrange("o p c d -> (o p) c d")).then_inc(s_we[k], 16)

            def expert_rows(e, k, fresh):
                if not fresh:
                    sp.wait_ge(s_xt, e - NW + 1)
                sp.dma_start(xe[:, k], xn_rows[bass.ds(e * CAP, CAP), :].rearrange("(c p) d -> p c d", p=SP_)).then_inc(s_xe[k], 16)

            for e in range(NW):
                expert_weights(e, e, True)
            sp.wait_ge(s_scat, 16 * B * TOPK)
            for e in range(NW):
                expert_rows(e, e, True)
            with sp.Fori(1, E // NW) as i:
                for k in range(NW):
                    expert_rows(i * NW + k, k, False)
                    expert_weights(i * NW + k, k, False)
            for b in range(B):
                sp.wait_ge(s_fin, b + 1)
                sp.dma_start(out[b], xn[0:S, b]).then_inc(s_out, 16)
            sp.wait_ge(s_out, 16 * B)

        @block.gpsimd
        def _(pool):
            link = [0]

            def chain(ins):
                link[0] += 1
                ins.then_inc(s_pool, 1)
                pool.wait_ge(s_pool, link[0])

            chain(nc.gpsimd.memset(ident[:], 0.0))
            nc.gpsimd.affine_select(out=ident[:], in_=ident[:], compare_op=ALU.not_equal, fill=1.0, base=0,
                                    pattern=[[-1, 128]], channel_multiplier=1).then_inc(s_ident, 1)
            nc.gpsimd.memset(y_out[:, 0, :], 0.0).then_inc(s_z, 1)
            chain(nc.gpsimd.memset(c_hi[:, :, KC - 1, :], 0.0))
            chain(nc.gpsimd.memset(c_lo[:, :, KC - 1, :], 0.0))

            def split(n, j, s_base):
                for k in range(PIECES):
                    loads = 16 * (n * (PIECES // 2 + (k % 2)) + k // 2 + 1) + (16 if k == PIECES - 1 else 0)
                    pool.wait_ge(s_raw[k % 2], loads)
                    pool.sem_inc(s_seen, 1)
                    if k < 4:
                        c, half = k // 2, k % 2
                        cols = slice(half * (KV // 2), (half + 1) * (KV // 2))
                        parts = [(raw[:, k % 2], ct_hi[:, j, c, cols], ct_lo[:, j, c, cols])]
                    else:
                        c = 2 * (k - 4)
                        src = raw[:, k % 2, 0:2 * D].rearrange("p (c d) -> p c d", c=2)
                        if c + 2 < KC:
                            parts = [(src[0:KP], c_hi[0:KP, j, c:c + 2], c_lo[0:KP, j, c:c + 2])]
                        else:
                            parts = [(src[0:r, m], c_hi[0:r, j, c + m], c_lo[0:r, j, c + m]) for m, r in enumerate((KP, KLAST))]
                    for src, hi, lo in parts:
                        last = nc.gpsimd.tensor_scalar(hi, src, F16MAX, -F16MAX, ALU.min, ALU.max)
                    last.then_inc(s_pool, 1)
                    pool.wait_ge(s_pool, s_base + n * PIECES + k + 1)
                    for src, hi, lo in parts:
                        last = nc.gpsimd.tensor_tensor(lo, src, hi, ALU.subtract)
                    last.then_inc(s_split, 1)

            s_base = link[0]
            split(0, 0, s_base)
            split(1, 1, s_base)
            with pool.Fori(1, PAIRS) as i:
                for j in range(2):
                    pool.wait_ge(s_yfull, 2 * i + j - 1)
                    split(2 * i + j, j, s_base)
            link[0] = s_base + B * PIECES

            pool.wait_ge(s_yfree, B + 1)
            nc.gpsimd.iota(iota_e[:], [[1, E]], base=0, channel_multiplier=0, allow_small_or_imprecise_dtypes=True).then_inc(s_const, 1)
            nc.gpsimd.iota(dump_row[:], [[1, B * TOPK]], base=DUMP, channel_multiplier=B * TOPK,
                           allow_small_or_imprecise_dtypes=True).then_inc(s_const, 1)
            nc.gpsimd.memset(ones[:], 1.0).then_inc(s_const, 1)
            chain(nc.gpsimd.memset(tri[:], 1.0))
            nc.gpsimd.affine_select(out=tri[:], in_=tri[:], compare_op=ALU.is_gt, fill=0.0, base=0,
                                    pattern=[[1, S]], channel_multiplier=-1).then_inc(s_const, 1)
            pool.wait_ge(s_slot, 1)
            pool.wait_ge(s_zero, 16)
            for b in range(B):
                for k in range(TOPK):
                    n = b * TOPK + k
                    nc.gpsimd.indirect_dma_start(xn_rows[:, :], bass.IndirectOffsetOnAxis(ap=scat_u[0:S, n:n + 1], axis=0),
                                                 xn[0:S, b, :], None).then_inc(s_scat, 16)
            pool.wait_ge(s_eost[0], 16 * (E // 2 + 1))
            pool.wait_ge(s_eost[1], 16 * (E // 2 + 1))
            for b in range(B):
                if b >= 2:
                    pool.wait_ge(s_comb, b - 1)
                for k in range(TOPK):
                    n = b * TOPK + k
                    nc.gpsimd.indirect_dma_start(back[0:S, b % 2, k, :], None, eo_rows[:, :],
                                                 bass.IndirectOffsetOnAxis(ap=slot_u[0:S, n:n + 1], axis=0)).then_inc(s_back[b % 2], 16)

        @block.scalar
        def _(sc):
            sc.sem_inc(s_exp, 1)
            sc.wait_ge(s_var, 1)
            nc.scalar.activation(std[0:S], rstd[0:S], ACT.Sqrt).then_inc(s_std, 1)
            sc.wait_ge(s_g, 32)
            nc.scalar.activation(gates[:, 2:4], gates[:, 0:2], ACT.Tanh).then_inc(s_tanh, 1)

            def high(n, dst, src, scale=1.0):
                sc.wait_ge(s_full, n + 1)
                nc.scalar.activation(dst, src, ACT.Copy, scale=scale).then_inc(s_hi, 1)

            for u in range(XFILLS):
                high(u, xt_hi[:, :, u * 2 * S:(u + 1) * 2 * S], stage[:, u % 2, 0:DC * 2 * S].rearrange("p (c t) -> p c t", c=DC))
            for which, dst in enumerate((m_hi, n_hi)):
                with sc.Fori(0, H // 2) as i:
                    for k in range(2):
                        high(XFILLS + which * H + 2 * i + k, dst[:, bass.ds(2 * i + k, 1)].rearrange("p o c d -> p (o c d)"), stage[:, k, :])

            with sc.Fori(0, PAIRS) as i:
                def fill_hi(f):
                    n = FILL[f]
                    src = stage[:, n % 2]
                    if f[0] == "q":
                        _, hp, c = f
                        high(SETUP_FILLS + i * FILLS + n,
                             q_hi[:, c, :, hp * 2 * S:(hp + 1) * 2 * S].rearrange("p j (h s) -> p j h s", h=2),
                             src[:, 0:4 * S].rearrange("p (h j s) -> p j h s", h=2, j=2))
                    else:
                        _, t, k = f
                        m = tile_rows(t)
                        off = 128 * (t % TILES - GROUPS[group_of(t)][0])
                        high(SETUP_FILLS + i * FILLS + n,
                             pt_hi[group_of(t) % 2][0:KP, 4 * k:4 * k + 4, off:off + m],
                             src[0:KP, :].rearrange("p (c q) -> p c q", c=4)[:, :, 0:m])

                for s in range(ALL_STEPS):
                    for hp, c in Q_FIRST.get(s, []):
                        fill_hi(("q", hp, c))
                    fills = fills_of_step(s)
                    for f in fills[:2]:
                        fill_hi(f)
                    if s < STEPS:
                        m = tile_rows(s)
                        sc.wait_ge(s_max, i * STEPS + s + 1)
                        nc.scalar.activation(probs[0:m, s % 2, 0:KV], scores[0:m, 0:KV], ACT.Exp,
                                             bias=neg_max[0:m, s % 2:s % 2 + 1], scale=1.0,
                                             accum_out=row_sum[0:m, s % 2:s % 2 + 1]).then_inc(s_exp, 1)
                    for f in fills[2:]:
                        fill_hi(f)
                    if s in PV and PV[s][3] == KC:
                        j, g, _, _ = PV[s]
                        w = group_width(g)
                        for c in range(DC):
                            sc.wait_ge(s_accfull, i * 2 * NG * DC + (j * NG + g) * DC + c + 1)
                            nc.scalar.activation(ut_hi[:, c, g * 256:g * 256 + w], acc[:, c, 0:w], ACT.Copy,
                                                 scale=1.0 / PSCALE).then_inc(s_uhi, 1)
                    if s in Y_STEP:
                        j = Y_STEP[s]
                        sc.wait_ge(s_yfree, 2 * i + j + 2)
                        sc.dma_start(attn_rows[bass.ds(2 * i + j, 1)].rearrange("o s d -> (o s) d"), y_out[0:S, j]).then_inc(s_yst[j], 16)

            sc.wait_ge(s_var2, 1)
            nc.scalar.activation(std[0:S], rstd[0:S], ACT.Sqrt).then_inc(s_std2, 1)
            for u in range(PAIRS):
                sc.wait_ge(s_tfull, u + 1)
                nc.scalar.activation(xnt[:, :, u * 2 * S:(u + 1) * 2 * S],
                                     stage[:, u % 2, 0:DC * 2 * S].rearrange("p (c t) -> p c t", c=DC), ACT.Copy).then_inc(s_tdone, 1)
            sc.wait_ge(s_nmx, 1)
            for b in range(B):
                last = nc.scalar.activation(ex[0:S, b], yps[0:S, b * E:(b + 1) * E], ACT.Exp, bias=nmx[0:S, b:b + 1], scale=1.0,
                                            accum_out=esum[0:S, b:b + 1])
            last.then_inc(s_ex, 1)
            for u in range(2 * FSC):
                sc.wait_ge(s_shup, u + 1)
                if u >= 2:
                    sc.wait_ge(s_shh, u - 1)
                nc.scalar.activation(sh_act[:, u % 2], ps[0:FP, u % 2, 0:NTOK // 2], ACT.Silu).then_inc(s_shact, 1)
            with sc.Fori(0, E // 2) as i:
                for k in range(2):
                    e = 2 * i + k
                    sc.wait_ge(s_xt, e + 1)
                    nc.scalar.activation(xet[:, k], stage[:, k, 0:DC * CAP].rearrange("p (c t) -> p c t", c=DC), ACT.Copy).then_inc(s_xtc, 1)
                for k in range(2):
                    e = 2 * i + k
                    sc.wait_ge(s_up, e + 1)
                    nc.scalar.activation(act[:, k], ps[0:FP, k, 0:FC * CAP].rearrange("p (c t) -> p c t", c=FC), ACT.Silu).then_inc(s_act, 1)
                for k in range(2):
                    e = 2 * i + k
                    sc.wait_ge(s_eo, e + 1)
                    sc.dma_start(eo_rows[bass.ds(e * CAP, CAP), :].rearrange("(c p) d -> p c d", p=SP_), eo[:, k]).then_inc(s_eost[k], 16)

        @block.vector
        def _(dve):
            link = [0]

            def chain(ins):
                link[0] += 1
                ins.then_inc(s_dve, 1)
                dve.wait_ge(s_dve, link[0])

            def moments(src, s_done):
                for b in range(B):
                    chain(nc.vector.bn_stats(stats[0:S, b], src[0:S, b]))
                    chain(nc.vector.bn_aggr(mean_var[0:S, b], stats[0:S, b]))
                nc.vector.tensor_scalar(rstd[0:S], mean_var[0:S, :, 1], EPS, None, ALU.add).then_inc(s_done, 1)

            def normalize(dst, src, scale, s_ready, s_done):
                dve.wait_ge(s_ready, 1)
                chain(nc.vector.reciprocal(rstd[0:S], std[0:S]))
                if scale != 1.0:
                    chain(nc.vector.tensor_scalar(rstd[0:S], rstd[0:S], scale, None, ALU.mult))
                for b in range(B):
                    nc.vector.tensor_scalar(dst[0:S, b], src[0:S, b], mean_var[0:S, b, 0:1], rstd[0:S, b:b + 1],
                                            ALU.subtract, ALU.mult).then_inc(s_done, 1)

            dve.sem_inc(s_accfree, 1)
            dve.sem_inc(s_yfree, 1)
            dve.wait_ge(s_x, 16)
            moments(x_in, s_var)
            normalize(x_norm, x_in, QSCALE, s_std, s_xnorm)

            def low(n, dst, src, hi):
                dve.wait_ge(s_hi, n + 1)
                nc.vector.tensor_tensor(dst, src, hi, ALU.subtract).then_inc(s_free, 1)

            for u in range(XFILLS):
                cols = slice(u * 2 * S, (u + 1) * 2 * S)
                low(u, xt_lo[:, :, cols], stage[:, u % 2, 0:DC * 2 * S].rearrange("p (c t) -> p c t", c=DC), xt_hi[:, :, cols])
            for which, (hi, lo) in enumerate(((m_hi, m_lo), (n_hi, n_lo))):
                with dve.Fori(0, H // 2) as i:
                    for k in range(2):
                        head = bass.ds(2 * i + k, 1)
                        low(XFILLS + which * H + 2 * i + k, lo[:, head].rearrange("p o c d -> p (o c d)"), stage[:, k, :],
                            hi[:, head].rearrange("p o c d -> p (o c d)"))
            nc.vector.memset(probs[:, :, KV:KPAD], 0.0).then_inc(s_pads, 1)
            dve.wait_ge(s_tanh, 1)

            with dve.Fori(0, PAIRS) as i:
                def fill_lo(f):
                    n = FILL[f]
                    src = stage[:, n % 2]
                    if f[0] == "q":
                        _, hp, c = f
                        part = lambda q: q[:, c, :, hp * 2 * S:(hp + 1) * 2 * S].rearrange("p j (h s) -> p j h s", h=2)
                        low(SETUP_FILLS + i * FILLS + n, part(q_lo), src[:, 0:4 * S].rearrange("p (h j s) -> p j h s", h=2, j=2), part(q_hi))
                    else:
                        _, t, k = f
                        m = tile_rows(t)
                        off = 128 * (t % TILES - GROUPS[group_of(t)][0])
                        part = lambda p: p[group_of(t) % 2][0:KP, 4 * k:4 * k + 4, off:off + m]
                        low(SETUP_FILLS + i * FILLS + n, part(pt_lo), src[0:KP, :].rearrange("p (c q) -> p c q", c=4)[:, :, 0:m], part(pt_hi))

                for s in range(ALL_STEPS):
                    for hp, c in Q_FIRST.get(s, []):
                        fill_lo(("q", hp, c))
                    if s < STEPS:
                        m = tile_rows(s)
                        dve.wait_ge(s_scores, i * STEPS + s + 1)
                        nc.vector.tensor_reduce(neg_max[0:m, s % 2:s % 2 + 1], scores[0:m, 0:KV], AX.X, ALU.max, negate=True).then_inc(s_max, 1)
                    fills = fills_of_step(s)
                    for f in fills[:3]:
                        fill_lo(f)
                    if s < STEPS:
                        dve.wait_ge(s_exp, i * STEPS + s + 2)
                        col = slice(s % 2, s % 2 + 1)
                        nc.vector.reciprocal(row_inv[0:m, col], row_sum[0:m, col]).then_inc(s_inv, 1)
                        dve.wait_ge(s_inv, i * STEPS + s + 1)
                        nc.vector.tensor_scalar(probs[0:m, s % 2, 0:KV], probs[0:m, s % 2, 0:KV], row_inv[0:m, col], PSCALE,
                                                ALU.mult, ALU.mult).then_inc(s_norm, 1)
                    for f in fills[3:]:
                        fill_lo(f)
                    if s in PV and PV[s][3] == KC:
                        j, g, _, _ = PV[s]
                        w = group_width(g)
                        for c in range(DC):
                            dve.wait_ge(s_uhi, i * 2 * NG * DC + (j * NG + g) * DC + c + 1)
                            cols = slice(g * 256, g * 256 + w)
                            nc.vector.scalar_tensor_tensor(out=ut_lo[:, c, cols], in0=acc[:, c, 0:w], scalar=1.0 / PSCALE, in1=ut_hi[:, c, cols],
                                                           op0=ALU.mult, op1=ALU.subtract).then_inc(s_accfree, 1)
                    if s in Y_STEP:
                        j = Y_STEP[s]
                        dve.wait_ge(s_yfull, 2 * i + j + 1)
                        dve.wait_ge(s_yst[j], 16 * (i + 1))
                        if j == 0:
                            dve.wait_ge(s_zero, 16)
                        nc.vector.tensor_scalar(y_out[0:S, j], yps[0:S, 0:D], gates[0:S, 2:3], None, ALU.mult).then_inc(s_yfree, 1)

            dve.wait_ge(s_res, 16)
            dve.wait_ge(s_att, 16)
            chain(nc.vector.tensor_tensor(x1[0:S], x1[0:S], xres[0:S], ALU.add))
            moments(x1, s_var2)
            normalize(xn, x1, 1.0, s_std2, s_xn2)
            dve.wait_ge(s_logit, 1)
            lg = yps[0:S, :].rearrange("p (b e) -> p b e", b=B)
            nc.vector.tensor_reduce(nmx[0:S], lg, AX.X, ALU.max, negate=True).then_inc(s_nmx, 1)
            dve.wait_ge(s_ex, 1)
            chain(nc.vector.reciprocal(esum[0:S], esum[0:S]))
            chain(nc.vector.tensor_tensor(ex[0:S], ex[0:S], esum[0:S].unsqueeze(2).to_broadcast([S, B, E]), ALU.mult))
            for b in range(B):
                chain(nc.vector.max(top[0:S, b], ex[0:S, b]))
                chain(nc.vector.max_index(topi[0:S, b], top[0:S, b], ex[0:S, b]))
            chain(nc.vector.tensor_reduce(wsum[0:S], top[0:S, :, 0:TOPK], AX.X, ALU.add))
            chain(nc.vector.tensor_scalar(wsum[0:S], wsum[0:S], 1e-20, None, ALU.add))
            chain(nc.vector.reciprocal(wsum[0:S], wsum[0:S]))
            chain(nc.vector.tensor_tensor(wk[0:S], top[0:S, :, 0:TOPK], wsum[0:S].unsqueeze(2).to_broadcast([S, B, TOPK]), ALU.mult))
            chain(nc.vector.tensor_copy(topf[0:S], topi[0:S, :, 0:TOPK]))
            dve.wait_ge(s_const, 4)
            hots = hot[0:S].rearrange("p b k e -> p (b k) e")
            chain(nc.vector.tensor_tensor(hots, iota_e[0:S].unsqueeze(1).to_broadcast([S, B * TOPK, E]),
                                          topf[0:S].rearrange("p b k -> p (b k)").unsqueeze(2).to_broadcast([S, B * TOPK, E]), ALU.is_equal))
            with nc.allow_low_precision("zeros and ones"):
                nc.vector.tensor_reduce(mask[0:S], hot[0:S].rearrange("p b k e -> p b e k"), AX.X, ALU.add).then_inc(s_mask, 1)
            dve.wait_ge(s_posps, 1)
            chain(nc.vector.tensor_copy(possb[0:S], lg))
            for b in range(B):
                chain(nc.vector.tensor_tensor(hotpos[0:S, b], hot[0:S, b], possb[0:S, b].unsqueeze(1).to_broadcast([S, TOPK, E]), ALU.mult))
            chain(nc.vector.tensor_reduce(pos[0:S], hotpos[0:S], AX.X, ALU.add))
            chain(nc.vector.tensor_scalar(over[0:S], pos[0:S], float(CAP), None, ALU.is_ge))
            chain(nc.vector.tensor_scalar(pos[0:S], pos[0:S], float(CAP - 1), None, ALU.min))
            chain(nc.vector.tensor_scalar(slot[0:S], topf[0:S], float(CAP), None, ALU.mult))
            chain(nc.vector.tensor_tensor(slot[0:S], slot[0:S], pos[0:S], ALU.add))
            chain(nc.vector.tensor_tensor(scat[0:S], dump_row[0:S], slot[0:S], ALU.subtract))
            chain(nc.vector.tensor_tensor(scat[0:S], scat[0:S], over[0:S], ALU.mult))
            chain(nc.vector.tensor_tensor(scat[0:S], scat[0:S], slot[0:S], ALU.add))
            chain(nc.vector.tensor_copy(scat_u[0:S], scat[0:S].rearrange("p b k -> p (b k)")))
            nc.vector.tensor_copy(slot_u[0:S], slot[0:S].rearrange("p b k -> p (b k)")).then_inc(s_slot, 1)
            chain(nc.vector.tensor_scalar(over[0:S], over[0:S], -1.0, 1.0, ALU.mult, ALU.add))
            chain(nc.vector.tensor_tensor(wk[0:S], wk[0:S], over[0:S], ALU.mult))
            for u in range(2 * FSC):
                fc, half = u // 2, u % 2
                dve.wait_ge(s_shact, u + 1)
                nc.vector.tensor_tensor(sh_h[:, fc, half * (NTOK // 2):(half + 1) * (NTOK // 2)], sh_act[:, u % 2],
                                        acc[0:FP, u % 2, 0:NTOK // 2], ALU.mult).then_inc(s_shh, 1)
            for b in range(B):
                dve.wait_ge(s_shdown, b + 1)
                nc.vector.tensor_copy(sh_out[0:S, b], (ps[0:S, 2, 0:D], yps[0:S, 0:D])[b % 2]).then_inc(s_shout, 1)
            with dve.Fori(0, E // 2) as i:
                for k in range(2):
                    e = 2 * i + k
                    dve.wait_ge(s_act, e + 1)
                    nc.vector.tensor_tensor(hid[:, k], act[:, k], acc[0:FP, k, 0:FC * CAP].rearrange("p (c t) -> p c t", c=FC),
                                            ALU.mult).then_inc(s_hid, 1)
                for k in range(2):
                    e = 2 * i + k
                    dve.wait_ge(s_down, e + 1)
                    dve.wait_ge(s_eost[k], 16 * (i + 1))
                    nc.vector.tensor_copy(eo[:, k].rearrange("p c d -> p (c d)"), (ps[0:SP_, 2], yps[0:SP_])[k]).then_inc(s_eo, 1)
            for b in range(B):
                dve.wait_ge(s_back[b % 2], 16 * TOPK * (b // 2 + 1))
                for k in range(TOPK):
                    ins = nc.vector.scalar_tensor_tensor(out=sh_out[0:S, b], in0=back[0:S, b % 2, k], scalar=wk[0:S, b, k:k + 1], in1=sh_out[0:S, b],
                                                         op0=ALU.mult, op1=ALU.add)
                    if k == TOPK - 1:
                        ins.then_inc(s_comb, 1)
                        dve.wait_ge(s_comb, b + 1)
                    else:
                        chain(ins)
                if b == 0:
                    dve.wait_ge(s_scat, 16 * B * TOPK)
                nc.vector.scalar_tensor_tensor(out=xn[0:S, b], in0=sh_out[0:S, b], scalar=gates[0:S, 3:4], in1=x1[0:S, b],
                                               op0=ALU.mult, op1=ALU.add).then_inc(s_fin, 1)

        @block.tensor
        def _(pe):
            def take(n):
                pe.wait_ge(s_free, n - 1)

            def products(dst, pairs, first=True, last=True):
                steps = [(l, r) for lh, ll, rh, rl in pairs for l, r in ((lh, rh), (lh, rl), (ll, rh))]
                for n, (l, r) in enumerate(steps):
                    ins = nc.tensor.matmul(dst, l, r, start=first and n == 0, stop=last and n == len(steps) - 1)
                return ins

            def transposes(src, n, s_done):
                for c in range(DC):
                    for j in range(2):
                        col = (c * 2 + j) * S
                        ins = nc.tensor.transpose(stage[:, n % 2, col:col + S], src[0:S, 2 * n + j, c * 128:(c + 1) * 128], ident[0:S, 0:S])
                ins.then_inc(s_done, 1)

            pe.wait_ge(s_ident, 1)
            for u in range(XFILLS):
                pe.wait_ge(s_xnorm, 2 * u + 2)
                if u >= 2:
                    take(u)
                transposes(x_norm, u, s_full)
            for which in range(2):
                with pe.Fori(0, QUADS // 2) as i:
                    for k in range(2):
                        pe.wait_ge(s_w[k], 32 * (which * 2 + i + 1))
                        for h in range(4):
                            n = XFILLS + which * H + (2 * i + k) * 4 + h
                            take(n)
                            for c in range(DC):
                                ins = nc.tensor.matmul(stage[:, h % 2, c * D:(c + 1) * D], w_raw[:, k, 0, h, c * 128:(c + 1) * 128],
                                                       w_raw[:, k, 1, h, :], start=True, stop=True)
                            if h == 3:
                                ins.then_inc(s_full, 1)
                                nc.tensor.transpose(yps[:, 0:128], ident[:], ident[:]).then_inc(s_wused, 1)
                            else:
                                ins.then_inc(s_full, 1)
            pe.wait_ge(s_pads, 1)

            with pe.Fori(0, PAIRS) as i:
                def q_fill(hp, c):
                    n = FILL[("q", hp, c)]
                    take(SETUP_FILLS + i * FILLS + n)
                    for h in range(2):
                        dst = stage[:, n % 2, h * 2 * S:(h + 1) * 2 * S]
                        cols = slice(c * 128, (c + 1) * 128)
                        ins = products(dst, [(m_hi[:, 2 * hp + h, k, cols], m_lo[:, 2 * hp + h, k, cols],
                                              xt_hi[:, k, bass.ds(i * 2 * S, 2 * S)], xt_lo[:, k, bass.ds(i * 2 * S, 2 * S)]) for k in range(DC)])
                    ins.then_inc(s_full, 1)

                def t_fill(t, k):
                    n = FILL[("T", t, k)]
                    if k == 0:
                        pe.wait_ge(s_norm, i * STEPS + t + 1)
                    take(SETUP_FILLS + i * FILLS + n)
                    for c in range(4):
                        ins = nc.tensor.transpose(stage[0:KP, n % 2, c * 128:(c + 1) * 128],
                                                  probs[:, t % 2, (4 * k + c) * KP:(4 * k + c + 1) * KP], ident[:])
                    ins.then_inc(s_full, 1)

                def weighted_sum(j, g, c0, c1):
                    w = group_width(g)
                    if c0 == 0:
                        pe.wait_ge(s_accfree, i * 2 * NG * DC + (j * NG + g) * DC + 1)
                        pe.wait_ge(s_free, SETUP_FILLS + i * FILLS + FILL[("T", j * TILES + GROUPS[g][-1], TBANKS - 1)] + 1)
                        if g == 0:
                            pe.wait_ge(s_split, (2 * i + j + 1) * PIECES)
                    for c in range(c0, c1):
                        for d in range(DC):
                            cols = slice(d * 128, (d + 1) * 128)
                            ins = products(acc[:, d, 0:w], [(c_hi[0:KP, j, c, cols], c_lo[0:KP, j, c, cols],
                                                             pt_hi[g % 2][0:KP, c, 0:w], pt_lo[g % 2][0:KP, c, 0:w])],
                                           first=c == 0, last=c == KC - 1)
                            if c == KC - 1:
                                ins.then_inc(s_accfull, 1)

                for s in range(ALL_STEPS):
                    for hp, c in Q_FIRST.get(s, []):
                        q_fill(hp, c)
                    if s < STEPS:
                        j, t = divmod(s, TILES)
                        m = tile_rows(s)
                        if t == 0:
                            pe.wait_ge(s_split, (2 * i + j) * PIECES + 4)
                        if s < 6:
                            pe.wait_ge(s_free, SETUP_FILLS + i * FILLS + FILL[("q", min(((s + 1) * 128 - 1) // (2 * S), H // 2 - 1), DC - 1)] + 1)
                        elif s == 6:
                            pe.wait_ge(s_free, SETUP_FILLS + i * FILLS + FILL[("q", H // 2 - 1, DC - 1)] + 1)
                        pe.wait_ge(s_exp, i * STEPS + s + 1)
                        rows = slice(t * 128, t * 128 + m)
                        for k0 in range(0, KV, 512):
                            k1 = min(k0 + 512, KV)
                            ins = products(scores[0:m, k0:k1], [(q_hi[:, c, j, rows], q_lo[:, c, j, rows],
                                                                 ct_hi[:, j, c, k0:k1], ct_lo[:, j, c, k0:k1]) for c in range(DC)])
                        ins.then_inc(s_scores, 1)
                    fills = fills_of_step(s)
                    for f in fills[:2]:
                        (q_fill if f[0] == "q" else t_fill)(*f[1:])
                    piece = PV.get(s)
                    if s == 27:
                        piece = None
                    if piece:
                        j, g, c0, c1 = piece
                        mid = (c0 + c1) // 2
                        weighted_sum(j, g, c0, mid)
                    for f in fills[2:]:
                        (q_fill if f[0] == "q" else t_fill)(*f[1:])
                    if s == 27:
                        j, g, c0, mid = PV[27][0], PV[27][1], PV[27][2], PV[27][2]
                        piece = PV[27]
                    if piece:
                        weighted_sum(j, g, mid, piece[3])
                    if s in Y_STEP:
                        j = Y_STEP[s]
                        pe.wait_ge(s_accfree, i * 2 * NG * DC + (j + 1) * NG * DC + 1)
                        pe.wait_ge(s_yfree, 2 * i + j + 1)
                        ins = products(yps[0:S, 0:D], [(ut_hi[:, c, h * S:(h + 1) * S], ut_lo[:, c, h * S:(h + 1) * S],
                                                        n_hi[:, h, c, :], n_lo[:, h, c, :]) for h in range(H) for c in range(DC)])
                        ins.then_inc(s_yfull, 1)

            for u in range(PAIRS):
                pe.wait_ge(s_xn2, 2 * u + 2)
                if u >= 2:
                    pe.wait_ge(s_tdone, u - 1)
                transposes(xn, u, s_tfull)
            pe.wait_ge(s_tdone, PAIRS)
            pe.wait_ge(s_fw, 64)
            for b in range(B):
                for c in range(DC):
                    ins = nc.tensor.matmul(yps[0:S, b * E:(b + 1) * E], xnt[:, c, b * S:(b + 1) * S], gate_w[:, c, :], start=c == 0, stop=c == DC - 1)
            ins.then_inc(s_logit, 1)
            def shared_up(u):
                fc, half = u // 2, u % 2
                toks = slice(half * (NTOK // 2), (half + 1) * (NTOK // 2))
                if u >= 2:
                    pe.wait_ge(s_shh, u - 1)
                for dst, w in ((ps[0:FP, u % 2], shg), (acc[0:FP, u % 2], shu)):
                    for c in range(DC):
                        ins = nc.tensor.matmul(dst[:, 0:NTOK // 2], w[:, c, fc * FP:(fc + 1) * FP], xnt[:, c, toks], start=c == 0, stop=c == DC - 1)
                ins.then_inc(s_shup, 1)

            for u in range(2):
                shared_up(u)
            pe.wait_ge(s_mask, 1)
            pe.wait_ge(s_const, 4)
            for b in range(B):
                for bb in range(b + 1):
                    ins = nc.tensor.matmul(yps[0:S, b * E:(b + 1) * E], (tri if bb == b else ones)[0:S, :], mask[0:S, bb, :], start=bb == 0, stop=bb == b)
            ins.then_inc(s_posps, 1)
            for u in range(2, 2 * FSC):
                shared_up(u)
            pe.wait_ge(s_shh, 2 * FSC)
            for b in range(B):
                if b >= 2:
                    pe.wait_ge(s_shout, b - 1)
                dst = (ps[0:S, 2, 0:D], yps[0:S, 0:D])[b % 2]
                for fc in range(FSC):
                    ins = nc.tensor.matmul(dst, sh_h[:, fc, b * S:(b + 1) * S], shd[:, fc, :], start=fc == 0, stop=fc == FSC - 1)
                ins.then_inc(s_shdown, 1)
            pe.wait_ge(s_shout, B)

            def rows_in(e, k, kw, wait_xe):
                pe.wait_ge(s_xe[kw], wait_xe)
                for c in range(DC):
                    for h in range(SC):
                        ins = nc.tensor.transpose(stage[:, k, c * CAP + h * SP_:c * CAP + (h + 1) * SP_],
                                                  xe[:, kw, h, c * 128:(c + 1) * 128], ident[0:SP_, 0:SP_])
                ins.then_inc(s_xt, 1)

            def up(e, k, kw, wait_w, guard):
                pe.wait_ge(s_we[kw], wait_w)
                pe.wait_ge(s_xtc, e + 1)
                if guard:
                    pe.wait_ge(s_hid, e - 1)
                for dst, w in ((ps[0:FP, k], wg), (acc[0:FP, k], wu)):
                    for fc in range(FC):
                        for c in range(DC):
                            ins = nc.tensor.matmul(dst[:, fc * CAP:(fc + 1) * CAP], w[:, kw, c, fc * FP:(fc + 1) * FP], xet[:, k, c, :],
                                                   start=c == 0, stop=c == DC - 1)
                ins.then_inc(s_up, 1)

            def down(e, k, kw, guard):
                pe.wait_ge(s_hid, e + 1)
                if guard:
                    pe.wait_ge(s_eo, e - 1)
                dst = (ps[0:SP_, 2], yps[0:SP_])[k]
                for h in range(SC):
                    for fc in range(FC):
                        ins = nc.tensor.matmul(dst[:, h * D:(h + 1) * D], hid[:, k, fc, h * SP_:(h + 1) * SP_], wd[:, kw, fc, :],
                                               start=fc == 0, stop=fc == FC - 1)
                ins.then_inc(s_down, 1)

            for k in range(2):
                rows_in(k, k, k, 16)

            def four(i, first, last):
                for h in range(2):
                    e0 = 4 * i + 2 * h
                    guard = not (first and h == 0)
                    for k in range(2):
                        up(e0 + k, k, 2 * h + k, 48 * (i + 1), guard)
                    if not (last and h == 1):
                        for k in range(2):
                            kw = (2 * h + 2 + k) % 4
                            rows_in(e0 + 2 + k, k, kw, 16 * (i + 1 + h))
                    for k in range(2):
                        down(e0 + k, k, 2 * h + k, guard)

            four(0, True, False)
            with pe.Fori(1, E // 4 - 1) as i:
                four(i, False, False)
            four(E // 4 - 1, False, True)


def kernel(**inputs):
    import numpy as _np
    import concourse.bacc as _bacc
    from concourse import mybir as _mybir
    from concourse.bass_utils import run_bass_kernel_spmd as _run

    a = {k: _np.asarray(v) for k, v in inputs.items()}

    def chunks(w, p):
        e, r, c = w.shape
        return w.reshape(e, r // p, p, c).transpose(0, 2, 1, 3)

    ins = {
        "x": a["x"],
        "ctx_rows": a["ctx_2048"],
        "ctx_cols": a["ctx_2048"].transpose(0, 2, 1),
        "wq_t": a["L0_xattn_Wq"].T,
        "wk_t": a["L0_xattn_Wk"].T,
        "wv_t": a["L0_xattn_Wv"].T,
        "wo": a["L0_xattn_Wo"],
        "g_xattn": a["g_xattn"],
        "g_ffn": a["g_ffn"],
        "gate_t": a["L0_ffn_gate_w"].T,
        "eg_t": chunks(a["L0_ffn_w_gate"].transpose(0, 2, 1), 128),
        "eu_t": chunks(a["L0_ffn_w_up"].transpose(0, 2, 1), 128),
        "ed_t": chunks(a["L0_ffn_w_down"].transpose(0, 2, 1), 88),
        "sg_t": a["L0_ffn_sh_gate"].T,
        "su_t": a["L0_ffn_sh_up"].T,
        "sd_t": a["L0_ffn_sh_down"].T,
    }
    nc = _bacc.Bacc("TRN2", target_bir_lowering=False, num_devices=1)
    arrays, args = {}, []
    for name, v in ins.items():
        v = _np.ascontiguousarray(v)
        arrays[f"in_{name}"] = v
        args.append(nc.dram_tensor(f"in_{name}", v.shape, _mybir.dt.from_np(v.dtype), kind="ExternalInput").ap())
    args.append(nc.dram_tensor("out_y", (8, 100, 256), _mybir.dt.float32, kind="ExternalOutput").ap())
    gated_cross_attention_moe(nc, *args)
    r = _run(nc, [arrays], core_ids=[0])
    return r.results[0]["out_y"]
```

```python
from contextlib import ExitStack

import numpy as np
import concourse.bass as bass
from concourse import mybir

ALU = mybir.AluOpType
ACT = mybir.ActivationFunctionType
AX = mybir.AxisListType
F32 = mybir.dt.float32
F16 = mybir.dt.float16
BF16 = mybir.dt.bfloat16
U32 = mybir.dt.uint32

B, S, D = 8, 100, 256
H, HD = 16, 128
KV = 1444
DC = D // 128
KC = 12
KP = -(-KV // KC)
KLAST = KV - (KC - 1) * KP
KPAD = KC * KP
Q = H * S
TILES = -(-Q // 128)
TLAST = Q - (TILES - 1) * 128
PAIRS = B // 2
EPS = 1e-5
QSCALE = float(HD) ** -0.5
PSCALE = 16384.0
F16MAX = 65504.0

E, F, FS, TOPK = 64, 176, 352, 6
NTOK = B * S
CAP = 2 * -(-NTOK * TOPK // E)
SC = 2
SP_ = CAP // SC
FP = 88
FC = F // FP
FSC = FS // FP
DUMP = E * CAP
SUMP = 95
assert (NTOK + CAP) % SUMP == 0 and DUMP == 128 * SP_
RW = D + 1 + E
UN = 8

STEPS = 2 * TILES
GROUPS = [(0, 1), (2, 3), (4, 5), (6, 7), (8, 9), (10, 11, 12)]
NG = len(GROUPS)


def tile_rows(t):
    return TLAST if t % TILES == TILES - 1 else 128


def group_of(t):
    return min((t % TILES) // 2, NG - 1)


def group_width(g):
    return sum(tile_rows(t) for t in GROUPS[g])


Q_FIRST = {0: [(0, 0), (0, 1)]}
Q_AFTER = {0: [1, 2], 1: [3, 4], 2: [5, 6], 3: [7]}
QFILLS = H // 2 * DC
TBANKS = KC // 4


def fills_of_step(s):
    out = []
    if 1 <= s <= STEPS:
        out += [("T", s - 1, k) for k in range(TBANKS)]
    for hp in Q_AFTER.get(s, []):
        out += [("q", hp, c) for c in range(DC)]
    return out


FILL = {}
for _s in range(STEPS + 1):
    for _f in [("q", hp, c) for hp, c in Q_FIRST.get(_s, [])] + fills_of_step(_s):
        FILL[_f] = len(FILL)
FILLS = len(FILL)
assert FILLS % 2 == 0 and FILLS == QFILLS + TBANKS * STEPS

PV = {}
for _j in range(2):
    _o = _j * TILES
    for _g in range(4):
        PV[_o + 2 * _g + 3] = (_j, _g, 0, 6)
        PV[_o + 2 * _g + 4] = (_j, _g, 6, 12)
    for _n in range(3):
        PV[_o + 11 + _n] = (_j, 4, 4 * _n, 4 * _n + 4)
    PV[_o + 14] = (_j, 5, 0, 6)
    PV[_o + 15] = (_j, 5, 6, 12)
Y_STEP = {16: 0, 28: 1}
ALL_STEPS = STEPS + 3
ROUTE_AT = {0: 17, 1: 1}
ROUTE_STAGES = 12
LINKS = {0: 2, 1: 2, 6: 4, 7: 5, 8: 2, 10: 3, 11: 7}
BATCH_LINKS = sum(LINKS.values())


def links_before(stage):
    return sum(n for at, n in LINKS.items() if at < stage)


def routing_at(step, first):
    out = []
    for j, start in ROUTE_AT.items():
        if 0 <= step - start < ROUTE_STAGES and not (j == 1 and first):
            out.append((-1 if j == 1 else 0, step - start))
    return out



XFILLS = PAIRS
assert XFILLS == 4 and H % 4 == 0
SETUP_FILLS = XFILLS + 2 * H
QUADS = H // 4
PIECES = 10


def gated_cross_attention_moe(nc, x, ctx_rows, ctx_cols, wq_t, wk_t, wv_t, wo, g_xattn, g_ffn, gate_t,
                              egu_t, ed_t, sg_t, su_t, sd_t, out):
    xn_rows = nc.dram_tensor("xn_rows", [DUMP + NTOK * TOPK, RW], F32, kind="Internal").ap()
    moe_sum = [nc.dram_tensor(f"moe_sum{n}", [NTOK + CAP, D], F32, kind="Internal").ap() for n in range(2)]
    x1_rows = nc.dram_tensor("x1_rows", [B, S, D], F32, kind="Internal").ap()
    xnt_cols = nc.dram_tensor("xnt_cols", [128, DC, NTOK], F32, kind="Internal").ap()

    stack = ExitStack()
    with stack:
        def sb(where, name, shape, dt=F32):
            return where.enter_context(nc.sbuf_tensor(name, shape, dt))

        def sem(name):
            return stack.enter_context(nc.semaphore(name))

        ps = stack.enter_context(nc.psum_tensor("ps", [128, 8, 512], F32))
        scores = ps[:, 0:3, :].rearrange("p a n -> p (a n)")
        stage = ps[:, 3:5, :]
        setup_bank = ps[:, 3:7, :]
        acc = ps[:, 5:7, :]
        yps = ps[:, 7, :]
        row_ps = yps[:, D:D + DC * S]
        logit_ps = yps[:, D:D + E]
        pos_ps = yps[:, D + 2 * E:D + 3 * E]

        ident = sb(stack, "ident", [128, 128])
        gates = sb(stack, "gates", [128, 4])
        stats = sb(stack, "stats", [128, B, 6])
        mean_var = sb(stack, "mean_var", [128, B, 2])
        rstd = sb(stack, "rstd", [128, B])
        std = sb(stack, "std", [128, B])
        x1_pair = sb(stack, "x1_pair", [128, 2, D])
        row = sb(stack, "row", [128, RW])
        row_t = sb(stack, "row_t", [128, DC, S])
        gate_w = sb(stack, "gate_w", [128, DC, E])
        ex = sb(stack, "ex", [128, E])
        nmx = sb(stack, "nmx", [128, 1])
        esum = sb(stack, "esum", [128, 1])
        top = sb(stack, "top", [128, 8])
        topi = sb(stack, "topi", [128, 8], U32)
        topf = sb(stack, "topf", [128, TOPK])
        wsum = sb(stack, "wsum", [128, 1])
        hot = sb(stack, "hot", [128, TOPK, E], BF16)
        hotpos = sb(stack, "hotpos", [128, TOPK, E])
        empty = hotpos[:].rearrange("p k e -> p (k e)").bitcast(U32)[0:E, 0:CAP]
        mask = sb(stack, "mask", [128, E], BF16)
        seen = sb(stack, "seen", [128, E], BF16)
        ones = sb(stack, "ones", [128, S], BF16)
        tri = sb(stack, "tri", [128, S], BF16)
        iota_e = sb(stack, "iota_e", [128, E])
        dump_row = sb(stack, "dump_row", [128, TOPK])
        minus_half = sb(stack, "minus_half", [128, 1])
        token_f = sb(stack, "token_f", [128, 1])
        pos = sb(stack, "pos", [128, TOPK])
        over = sb(stack, "over", [128, TOPK])
        slot = sb(stack, "slot", [128, TOPK])
        scat = sb(stack, "scat", [128, TOPK])
        scat_u = sb(stack, "scat_u", [128, TOPK], U32)

        attn = ExitStack()
        xt_hi = sb(attn, "xt_hi", [128, DC, NTOK], F16)
        xt_lo = sb(attn, "xt_lo", [128, DC, NTOK], BF16)
        m_hi = sb(attn, "m_hi", [128, H, DC, D], F16)
        m_lo = sb(attn, "m_lo", [128, H, DC, D], BF16)
        n_hi = sb(attn, "n_hi", [128, H, DC, D], F16)
        n_lo = sb(attn, "n_lo", [128, H, DC, D], BF16)
        q_hi = sb(attn, "q_hi", [128, DC, 2, Q], F16)
        q_lo = sb(attn, "q_lo", [128, DC, 2, Q], BF16)
        ct_hi = sb(attn, "ct_hi", [128, 2, DC, KV], F16)
        ct_lo = sb(attn, "ct_lo", [128, 2, DC, KV], BF16)
        c_hi = sb(attn, "c_hi", [128, 2, KC, D], F16)
        c_lo = sb(attn, "c_lo", [128, 2, KC, D], BF16)
        raw = sb(attn, "raw", [128, 2, KV // 2])
        neg_max = sb(attn, "neg_max", [128, 2])
        row_sum = sb(attn, "row_sum", [128, 2])
        row_inv = sb(attn, "row_inv", [128, 2])
        setup = ExitStack()
        x_in = sb(setup, "x_in", [128, B, D])
        x_norm = sb(setup, "x_norm", [128, B, D])
        w_raw = sb(setup, "w_raw", [128, 2, 2, 4, D])
        setup.close()
        probs = sb(attn, "probs", [128, 2, KPAD])
        pt_hi = [sb(attn, f"pt_hi{n}", [128, KC, group_width(4 + n)], F16) for n in range(2)]
        pt_lo = [sb(attn, f"pt_lo{n}", [128, KC, group_width(4 + n)], BF16) for n in range(2)]
        ut_hi = sb(attn, "ut_hi", [128, DC, Q], F16)
        ut_lo = sb(attn, "ut_lo", [128, DC, Q], BF16)
        attn.close()

        ffn = ExitStack()
        x1 = sb(ffn, "x1", [128, B, D])
        result = sb(ffn, "result", [128, B, D])
        xnt = sb(ffn, "xnt", [128, DC, NTOK])
        shg = sb(ffn, "shg", [128, DC, FS])
        shu = sb(ffn, "shu", [128, DC, FS])
        shd = sb(ffn, "shd", [FP, FSC, D])
        sh_act = sb(ffn, "sh_act", [FP, 2, NTOK // 2])
        sh_h = sb(ffn, "sh_h", [FP, FSC, NTOK])
        NW = 4
        wgu = sb(ffn, "wgu", [128, NW, DC, 2 * F])
        wgu_hi = sb(ffn, "wgu_hi", [128, NW, DC, 2 * F], F16)
        wgu_lo = sb(ffn, "wgu_lo", [128, NW, DC, 2 * F], BF16)
        wd = sb(ffn, "wd", [FP, NW, FC, D])
        wd_hi = sb(ffn, "wd_hi", [FP, NW, FC, D], F16)
        wd_lo = sb(ffn, "wd_lo", [FP, NW, FC, D], BF16)
        xe = sb(ffn, "xe", [SP_, UN, SC, D + 1 + UN])
        xet_hi = sb(ffn, "xet_hi", [128, 2, DC, CAP], F16)
        xet_lo = sb(ffn, "xet_lo", [128, 2, DC, CAP], BF16)
        act = sb(ffn, "act", [FP, 2, FC, CAP])
        hid = sb(ffn, "hid", [FP, 2, FC, CAP])
        hid_hi = sb(ffn, "hid_hi", [FP, 2, FC, CAP], F16)
        hid_lo = sb(ffn, "hid_lo", [FP, 2, FC, CAP], BF16)
        eo = sb(ffn, "eo", [SP_, 2, SC, D])
        back = sb(ffn, "back", [128, 2, B, D])
        ffn.close()

        s_x, s_g, s_ident = sem("s_x"), sem("s_g"), sem("s_ident")
        s_dve, s_pool = sem("s_dve"), sem("s_pool")
        s_var, s_std, s_xnorm, s_tanh = sem("s_var"), sem("s_std"), sem("s_xnorm"), sem("s_tanh")
        s_w = [sem("s_w0"), sem("s_w1")]
        s_wused = sem("s_wused")
        s_full, s_hi, s_free = sem("s_full"), sem("s_hi"), sem("s_free")
        s_scores, s_max, s_exp, s_inv, s_norm = (sem(n) for n in ("s_scores", "s_max", "s_exp", "s_inv", "s_norm"))
        s_accfull, s_uhi, s_accfree = sem("s_accfull"), sem("s_uhi"), sem("s_accfree")
        s_yfull, s_yfree = sem("s_yfull"), sem("s_yfree")
        s_yst = [sem("s_yst0"), sem("s_yst1")]
        s_raw = [sem("s_raw0"), sem("s_raw1")]
        s_split = sem("s_split")
        s_pads, s_seen = sem("s_pads"), sem("s_seen")
        s_z, s_zero = sem("s_z"), sem("s_zero")
        s_xin = [sem("s_xin0"), sem("s_xin1")]
        s_res, s_gw, s_fw, s_xnt = sem("s_res"), sem("s_gw"), sem("s_fw"), sem("s_xnt")
        s_row, s_rowps, s_rowt, s_rowst = sem("s_row"), sem("s_rowps"), sem("s_rowt"), sem("s_rowst")
        s_logit, s_nmx, s_ex, s_pos, s_slot, s_scat = (sem(n) for n in ("s_logit", "s_nmx", "s_ex", "s_pos", "s_slot", "s_scat"))
        s_moments, s_scale = sem("s_moments"), sem("s_scale")
        s_route = sem("s_route")
        s_dseen, s_lseen = sem("s_dseen"), sem("s_lseen")
        s_const = sem("s_const")
        s_shup, s_shact, s_shh, s_shdown, s_shout = (sem(n) for n in ("s_shup", "s_shact", "s_shh", "s_shdown", "s_shout"))
        s_we = [sem(f"s_we{n}") for n in range(4)]
        s_xe = [sem(f"s_xe{n}") for n in range(UN)]
        s_guhi, s_wdhi, s_gulo, s_wlo = sem("s_guhi"), sem("s_wdhi"), sem("s_gulo"), sem("s_wlo")
        s_xt, s_xhi, s_xlo = sem("s_xt"), sem("s_xhi"), sem("s_xlo")
        s_up, s_act, s_hid, s_hhi, s_hlo, s_down, s_eo = (sem(n) for n in ("s_up", "s_act", "s_hid", "s_hhi", "s_hlo", "s_down", "s_eo"))
        s_add = [sem("s_add0"), sem("s_add1")]
        s_back = [sem("s_back0"), sem("s_back1")]
        s_out, s_fin = sem("s_out"), sem("s_fin")

        xr = x.rearrange("b s d -> s b d")
        heads4 = lambda w, n: w[bass.ds(n * 4 * HD, 4 * HD), :].rearrange("(h p) d -> p h d", p=HD)

        block = stack.enter_context(nc.Block())

        @block.sync
        def _(sp):
            sp.dma_start(x_in[0:S, :, :], xr).then_inc(s_x, 16)
            sp.dma_start(gates[:, 0:1], g_xattn.partition_broadcast(128)).then_inc(s_g, 16)
            sp.dma_start(gates[:, 1:2], g_ffn.partition_broadcast(128)).then_inc(s_g, 16)

            def weights(n):
                first, second = ((wq_t, wk_t), (wv_t, wo))[n // QUADS]
                if n >= 2:
                    sp.wait_ge(s_wused, n - 1)
                sp.dma_start(w_raw[:, n % 2, 0], heads4(first, n % QUADS)).then_inc(s_w[n % 2], 16)
                sp.dma_start(w_raw[:, n % 2, 1], heads4(second, n % QUADS)).then_inc(s_w[n % 2], 16)

            def context(n, fresh, pieces=range(PIECES)):
                for k in pieces:
                    if not (fresh and k < 2):
                        sp.wait_ge(s_split, n * PIECES + k - 1)
                    dst = raw[:, k % 2]
                    if k < 4:
                        c, half = k // 2, k % 2
                        sp.dma_start(dst, ctx_cols[bass.ds(n, 1), c * 128:(c + 1) * 128, half * (KV // 2):(half + 1) * (KV // 2)]
                                     .rearrange("o p n -> (o p) n")).then_inc(s_raw[k % 2], 16)
                    else:
                        c = 2 * (k - 4)
                        dst = dst[:, 0:2 * D].rearrange("p (c d) -> p c d", c=2)
                        src = ctx_rows[bass.ds(n, 1), :, :].rearrange("o n d -> (o n) d")
                        if c + 2 < KC:
                            sp.dma_start(dst[0:KP], src[c * KP:(c + 2) * KP, :].rearrange("(c p) d -> p c d", p=KP)).then_inc(s_raw[k % 2], 16)
                        else:
                            sp.dma_start(dst[0:KP, 0], src[c * KP:(c + 1) * KP, :]).then_inc(s_raw[k % 2], 16)
                            sp.dma_start(dst[0:KLAST, 1], src[(c + 1) * KP:KV, :]).then_inc(s_raw[k % 2], 16)

            weights(0)
            context(0, True, [0])
            weights(1)
            context(0, True, [1, 2, 3])
            for n in range(2, 2 * QUADS):
                weights(n)
                context(0, False, [n + 2])
            context(1, False)
            sp.wait_ge(s_z, 2)
            groups = xn_rows[0:DUMP].rearrange("(p r) d -> p r d", p=128)
            sp.dma_start(groups[:, :, 0:D], row[:, 0:D].unsqueeze(1).to_broadcast([128, SP_, D])).then_inc(s_zero, 16)
            sp.dma_start(groups[:, :, D + 1:RW], row[:, 0:E].unsqueeze(1).to_broadcast([128, SP_, E])).then_inc(s_zero, 16)
            sp.dma_start(xn_rows[0:DUMP, D:D + 1].rearrange("(p r) d -> p (r d)", p=E), empty.bitcast(F32), allow_slow_non_contiguous=True).then_inc(s_zero, 16)
            for n in range(2):
                sp.dma_start(moe_sum[n].rearrange("(p r) d -> p r d", p=SUMP),
                             row[0:SUMP, 0:D].unsqueeze(1).to_broadcast([SUMP, (NTOK + CAP) // SUMP, D])).then_inc(s_zero, 16)
            sp.dma_start(gate_w[:], gate_t.rearrange("(c p) e -> p c e", p=128)).then_inc(s_gw, 16)
            for j in range(2):
                sp.dma_start(x1_pair[0:S, j], x[j]).then_inc(s_xin[j], 16)
            with sp.Fori(1, PAIRS) as i:
                for j in range(2):
                    context(2 * i + j, False)
                    sp.wait_ge(s_yst[j], 16 * i)
                    sp.sem_inc(s_lseen, 1)
                    sp.wait_ge(s_row, 2 * i + j - 1)
                    sp.sem_inc(s_lseen, 1)
                    sp.dma_start(x1_pair[0:S, j], x[bass.ds(2 * i + j, 1)].rearrange("o s d -> (o s) d")).then_inc(s_xin[j], 16)

            sp.wait_ge(s_yfree, B + 1)
            sp.dma_start(shg[:], sg_t.rearrange("(c p) f -> p c f", p=128)).then_inc(s_fw, 16)
            sp.dma_start(shu[:], su_t.rearrange("(c p) f -> p c f", p=128)).then_inc(s_fw, 16)
            sp.wait_ge(s_rowst, 16 * (B - 1))
            sp.dma_start(xnt[:, :, 0:(B - 1) * S], xnt_cols[:, :, 0:(B - 1) * S]).then_inc(s_xnt, 16)
            sp.dma_start(shd[:], sd_t.rearrange("(c p) d -> p c d", p=FP)).then_inc(s_fw, 16)

            def expert_weights(e, k, fresh):
                if not fresh:
                    sp.wait_ge(s_wlo, e - NW + 1)
                one = lambda w: w[bass.ds(e, 1)]
                sp.dma_start(wgu[:, k], one(egu_t).rearrange("o p c f -> (o p) c f")).then_inc(s_we[k], 16)
                sp.dma_start(wd[:, k], one(ed_t).rearrange("o p c d -> (o p) c d")).then_inc(s_we[k], 16)

            def expert_rows(e, k, turn, adds, fresh):
                if not fresh:
                    sp.wait_ge(s_add[k % 2], adds)
                src = xn_rows[bass.ds(e * CAP, CAP), :].rearrange("(c p) d -> p c d", p=SP_)
                sp.dma_start(xe[:, k, :, 0:D + 1], src[:, :, 0:D + 1]).then_inc(s_xe[k], 16)
                sp.dma_start(xe[:, k, :, D + 1:D + 1 + UN],
                             xn_rows[bass.ds(e * CAP, CAP), bass.ds(D + 1 + turn * UN, UN)].rearrange("(c p) d -> p c d", p=SP_)).then_inc(s_xe[k], 16)

            for e in range(NW):
                expert_weights(e, e, True)
            for k in range(2):
                sp.wait_ge(s_yst[k], 16 * PAIRS)
            sp.dma_start(x1[0:S], x1_rows.rearrange("b s d -> s b d")).then_inc(s_res, 16)
            for e in range(NW, NW + 2):
                expert_weights(e, e % NW, False)
            sp.wait_ge(s_scat, 16 * B * TOPK)
            for e in range(UN):
                expert_rows(e, e, 0, None, True)
            for e in range(NW + 2, UN):
                expert_weights(e, e % NW, False)
            with sp.Fori(1, E // UN) as i:
                for k in range(UN):
                    expert_weights(i * UN + k, k % NW, False)
                    expert_rows(i * UN + k, k, i, 16 * SC * ((i - 1) * (UN // 2) + k // 2 + 1), False)
            for k in range(2):
                sp.wait_ge(s_add[k], 16 * SC * (E // 2))
            for half in range(2):
                for n in range(2):
                    sp.dma_start(back[0:S, n, half * (B // 2):(half + 1) * (B // 2)],
                                 moe_sum[n][half * (NTOK // 2):(half + 1) * (NTOK // 2), :].rearrange("(b s) d -> s b d", s=S)).then_inc(s_back[half], 16)
            for half in range(2):
                bs = slice(half * (B // 2), (half + 1) * (B // 2))
                sp.wait_ge(s_fin, half + 1)
                sp.dma_start(out[bs].rearrange("b s d -> s b d"), result[0:S, bs]).then_inc(s_out, 16)
            sp.wait_ge(s_out, 32)

        @block.gpsimd
        def _(pool):
            link = [0]

            def chain(ins):
                link[0] += 1
                ins.then_inc(s_pool, 1)
                pool.wait_ge(s_pool, link[0])

            chain(nc.gpsimd.memset(ident[:], 0.0))
            nc.gpsimd.affine_select(out=ident[:], in_=ident[:], compare_op=ALU.not_equal, fill=1.0, base=0,
                                    pattern=[[-1, 128]], channel_multiplier=1).then_inc(s_ident, 1)
            nc.gpsimd.memset(row[:], 0.0).then_inc(s_z, 1)
            nc.gpsimd.iota(empty, [[1, CAP]], base=NTOK, channel_multiplier=0).then_inc(s_z, 1)
            chain(nc.gpsimd.memset(c_hi[:, :, KC - 1, :], 0.0))
            chain(nc.gpsimd.memset(c_lo[:, :, KC - 1, :], 0.0))

            def split(n, j, s_base):
                for k in range(PIECES):
                    loads = 16 * (n * (PIECES // 2 + (k % 2)) + k // 2 + 1) + (16 if k == PIECES - 1 else 0)
                    pool.wait_ge(s_raw[k % 2], loads)
                    pool.sem_inc(s_seen, 1)
                    if k < 4:
                        c, half = k // 2, k % 2
                        cols = slice(half * (KV // 2), (half + 1) * (KV // 2))
                        parts = [(raw[:, k % 2], ct_hi[:, j, c, cols], ct_lo[:, j, c, cols])]
                    else:
                        c = 2 * (k - 4)
                        src = raw[:, k % 2, 0:2 * D].rearrange("p (c d) -> p c d", c=2)
                        if c + 2 < KC:
                            parts = [(src[0:KP], c_hi[0:KP, j, c:c + 2], c_lo[0:KP, j, c:c + 2])]
                        else:
                            parts = [(src[0:r, m], c_hi[0:r, j, c + m], c_lo[0:r, j, c + m]) for m, r in enumerate((KP, KLAST))]
                    for src, hi, lo in parts:
                        last = nc.gpsimd.tensor_scalar(hi, src, F16MAX, -F16MAX, ALU.min, ALU.max)
                    last.then_inc(s_pool, 1)
                    pool.wait_ge(s_pool, s_base + n * PIECES + k + 1)
                    for src, hi, lo in parts:
                        last = nc.gpsimd.tensor_tensor(lo, src, hi, ALU.subtract)
                    last.then_inc(s_split, 1)

            def scale(b):
                pool.wait_ge(s_moments, b + 1)
                pool.sem_inc(s_seen, 1)
                nc.gpsimd.tensor_tensor(rstd[0:S, 0:1], std[0:S, 0:1], minus_half[0:S], ALU.pow).then_inc(s_scale, 1)

            def dispatch(b):
                if not (isinstance(b, int) and b == B - 1):
                    pool.wait_ge(s_rowt, b + 1)
                    pool.sem_inc(s_seen, 1)
                    pool.dma_start(xnt_cols[:, :, bass.ds(b * S, S)], row_t[:]).then_inc(s_rowst, 16)
                pool.wait_ge(s_slot, b + 1)
                pool.sem_inc(s_seen, 1)
                for k in range(TOPK):
                    nc.gpsimd.indirect_dma_start(xn_rows[:, :], bass.IndirectOffsetOnAxis(ap=scat_u[0:S, k:k + 1], axis=0),
                                                 row[0:S], None).then_inc(s_scat, 16)

            s_base = link[0]
            split(0, 0, s_base)
            split(1, 1, s_base)
            nc.gpsimd.iota(iota_e[:], [[1, E]], base=0, channel_multiplier=0, allow_small_or_imprecise_dtypes=True).then_inc(s_const, 1)
            nc.gpsimd.iota(dump_row[:], [[1, TOPK]], base=DUMP, channel_multiplier=TOPK,
                           allow_small_or_imprecise_dtypes=True).then_inc(s_const, 1)
            nc.gpsimd.iota(token_f[:], [[1, 1]], base=0, channel_multiplier=1, allow_small_or_imprecise_dtypes=True).then_inc(s_const, 1)
            nc.gpsimd.memset(seen[:], 0.0).then_inc(s_const, 1)
            nc.gpsimd.memset(minus_half[:], -0.5).then_inc(s_const, 1)
            nc.gpsimd.memset(ones[:], 1.0).then_inc(s_const, 1)
            nc.gpsimd.memset(tri[:], 1.0).then_inc(s_pool, 1)
            link[0] += 1
            pool.wait_ge(s_pool, s_base + 2 * PIECES + 1)
            nc.gpsimd.affine_select(out=tri[:], in_=tri[:], compare_op=ALU.is_gt, fill=0.0, base=0,
                                    pattern=[[1, S]], channel_multiplier=-1).then_inc(s_const, 1)
            with pool.Fori(1, PAIRS) as i:
                for j in range(2):
                    pool.wait_ge(s_yfull, 2 * i + j - 1)
                    scale(2 * i + j - 2)
                    split(2 * i + j, j, s_base + 1)
                    dispatch(2 * i + j - 2)
            for b in range(B - 2, B):
                scale(b)
                dispatch(b)

            def add_rows(e, k, adds):
                pool.wait_ge(s_eo, e + 1)
                if adds is not None:
                    pool.wait_ge(s_add[k % 2], adds)
                pool.sem_inc(s_seen, 1)
                for h in range(SC):
                    nc.gpsimd.indirect_dma_start(moe_sum[k % 2][:, :], bass.IndirectOffsetOnAxis(ap=xe[:, k, h, D:D + 1].bitcast(U32), axis=0),
                                                 eo[:, k % 2, h, :], None, compute_op=ALU.add).then_inc(s_add[k % 2], 16)

            for e in range(UN):
                add_rows(e, e, None if e < 2 else 16 * SC * (e // 2))
            with pool.Fori(1, E // UN) as i:
                for k in range(UN):
                    add_rows(UN * i + k, k, 16 * SC * (i * (UN // 2) + k // 2))

        @block.scalar
        def _(sc):
            sc.sem_inc(s_exp, 1)
            sc.wait_ge(s_var, 1)
            nc.scalar.activation(std[0:S], rstd[0:S], ACT.Sqrt).then_inc(s_std, 1)
            sc.wait_ge(s_g, 32)
            nc.scalar.activation(gates[:, 2:4], gates[:, 0:2], ACT.Tanh).then_inc(s_tanh, 1)

            def high(n, dst, src, scale=1.0):
                sc.wait_ge(s_full, n + 1)
                nc.scalar.activation(dst, src, ACT.Copy, scale=scale).then_inc(s_hi, 1)

            for u in range(XFILLS):
                high(u, xt_hi[:, :, u * 2 * S:(u + 1) * 2 * S], setup_bank[:, u, 0:DC * 2 * S].rearrange("p (c t) -> p c t", c=DC))
            for which, dst in enumerate((m_hi, n_hi)):
                with sc.Fori(0, H // 4) as i:
                    for k in range(4):
                        high(XFILLS + which * H + 4 * i + k, dst[:, bass.ds(4 * i + k, 1)].rearrange("p o c d -> p (o c d)"), setup_bank[:, k, :])

            def route(b, stage_no, dst=row_t[:]):
                if stage_no == 2:
                    sc.wait_ge(s_rowps, b + 1)
                    if not isinstance(b, int) or 0 < b < B - 1:
                        sc.wait_ge(s_rowst, 16 * b)
                    nc.scalar.activation(dst, row_ps.rearrange("p (c t) -> p c t", c=DC), ACT.Copy).then_inc(s_rowt, 1)
                elif stage_no == 5:
                    sc.wait_ge(s_nmx, b + 1)
                    nc.scalar.activation(ex[0:S], logit_ps[0:S], ACT.Exp, bias=nmx[0:S], scale=1.0, accum_out=esum[0:S]).then_inc(s_ex, 1)

            def pair(i, first):
                def fill_hi(f):
                    n = FILL[f]
                    src = stage[:, n % 2]
                    if f[0] == "q":
                        _, hp, c = f
                        high(SETUP_FILLS + i * FILLS + n,
                             q_hi[:, c, :, hp * 2 * S:(hp + 1) * 2 * S].rearrange("p j (h s) -> p j h s", h=2),
                             src[:, 0:4 * S].rearrange("p (h j s) -> p j h s", h=2, j=2))
                    else:
                        _, t, k = f
                        m = tile_rows(t)
                        off = 128 * (t % TILES - GROUPS[group_of(t)][0])
                        high(SETUP_FILLS + i * FILLS + n,
                             pt_hi[group_of(t) % 2][0:KP, 4 * k:4 * k + 4, off:off + m],
                             src[0:KP, :].rearrange("p (c q) -> p c q", c=4)[:, :, 0:m])

                for s in range(ALL_STEPS):
                    for hp, c in Q_FIRST.get(s, []):
                        fill_hi(("q", hp, c))
                    fills = fills_of_step(s)
                    for f in fills[:2]:
                        fill_hi(f)
                    if s < STEPS:
                        m = tile_rows(s)
                        sc.wait_ge(s_max, i * STEPS + s + 1)
                        nc.scalar.activation(probs[0:m, s % 2, 0:KV], scores[0:m, 0:KV], ACT.Exp,
                                             bias=neg_max[0:m, s % 2:s % 2 + 1], scale=1.0,
                                             accum_out=row_sum[0:m, s % 2:s % 2 + 1]).then_inc(s_exp, 1)
                    for f in fills[2:]:
                        fill_hi(f)
                    if s in PV and PV[s][3] == KC:
                        j, g, _, _ = PV[s]
                        w = group_width(g)
                        for c in range(DC):
                            sc.wait_ge(s_accfull, i * 2 * NG * DC + (j * NG + g) * DC + c + 1)
                            nc.scalar.activation(ut_hi[:, c, g * 256:g * 256 + w], acc[:, c, 0:w], ACT.Copy,
                                                 scale=1.0 / PSCALE).then_inc(s_uhi, 1)
                    if s in Y_STEP:
                        j = Y_STEP[s]
                        sc.wait_ge(s_yfree, 2 * i + j + 2)
                        sc.dma_start(x1_rows[bass.ds(2 * i + j, 1)].rearrange("o s d -> (o s) d"), x1_pair[0:S, j]).then_inc(s_yst[j], 16)
                    for j, stage_no in routing_at(s, first):
                        route(2 * i + j, stage_no)

            pair(0, True)
            with sc.Fori(1, PAIRS) as i:
                pair(i, False)

            route(B - 1, 2, xnt[:, :, (B - 1) * S:NTOK])
            for u in range(2 * FSC):
                sc.wait_ge(s_shup, u + 1)
                if u >= 2:
                    sc.wait_ge(s_shh, u - 1)
                nc.scalar.activation(sh_act[:, u % 2], ps[0:FP, u % 2, 0:NTOK // 2], ACT.Silu).then_inc(s_shact, 1)
                if u == 0:
                    route(B - 1, 5)

            def up_high(k, load, used):
                sc.wait_ge(s_we[k], load)
                if used is not None:
                    sc.wait_ge(s_up, used)
                nc.scalar.activation(wgu_hi[:, k], wgu[:, k], ACT.Copy).then_inc(s_guhi, 1)

            def down_high(k, used):
                if used is not None:
                    sc.wait_ge(s_down, used)
                nc.scalar.activation(wd_hi[:, k], wd[:, k], ACT.Copy).then_inc(s_wdhi, 1)

            def rows_high(e, k2):
                sc.wait_ge(s_xt, e + 1)
                nc.scalar.activation(xet_hi[:, k2], stage[:, k2, 0:DC * CAP].rearrange("p (c t) -> p c t", c=DC), ACT.Copy).then_inc(s_xhi, 1)

            def gate(e, k2):
                sc.wait_ge(s_up, e + 1)
                nc.scalar.activation(act[:, k2], ps[0:FP, k2, 0:FC * CAP].rearrange("p (c t) -> p c t", c=FC), ACT.Silu).then_inc(s_act, 1)

            def hidden_high(e, k2):
                sc.wait_ge(s_hid, e + 1)
                nc.scalar.activation(hid_hi[:, k2], hid[:, k2], ACT.Copy).then_inc(s_hhi, 1)

            def expert_out(e, k, adds):
                k2 = k % 2
                sc.wait_ge(s_down, e + 1)
                if adds is not None:
                    sc.wait_ge(s_add[k2], adds)
                for h in range(SC):
                    ins = nc.scalar.activation(eo[:, k2, h], (ps[0:SP_, 2], yps[0:SP_])[k2][:, h * D:(h + 1) * D], ACT.Copy,
                                               scale=xe[:, k, h, D + 1 + k:D + 2 + k])
                ins.then_inc(s_eo, 1)

            def turn(i, first, last):
                for k in range(UN):
                    e, k2 = UN * i + k, k % 2
                    if not (last and k == UN - 1):
                        rows_high(e + 1, (k + 1) % 2)
                    if not (first and k < 2):
                        expert_out(e - 2, (k - 2) % UN, None if first and k < 4 else 16 * SC * (i * (UN // 2) + k // 2 - 1))
                    if not (last and k >= UN - 2):
                        down_high((k + 2) % NW, None if first and k < 2 else e - 1)
                    gate(e, k2)
                    if not (last and k >= UN - 3):
                        up_high((k + 3) % NW, 32 * (i * (UN // NW) + (k + 3) // NW + 1), None if first and k < 1 else e)
                    hidden_high(e, k2)

            for e in range(3):
                up_high(e, 32, None)
                if e < 2:
                    down_high(e, None)
            rows_high(0, 0)
            turn(0, True, False)
            with sc.Fori(1, E // UN - 1) as i:
                turn(i, False, False)
            turn(E // UN - 1, False, True)
            for e in range(E - 2, E):
                expert_out(e, e % UN, 16 * SC * (E // 2 - 1))

        @block.vector
        def _(dve):
            link = [0]

            def chain(ins):
                link[0] += 1
                ins.then_inc(s_dve, 1)
                dve.wait_ge(s_dve, link[0])

            def moments(src, s_done):
                for b in range(B):
                    chain(nc.vector.bn_stats(stats[0:S, b], src[0:S, b]))
                    chain(nc.vector.bn_aggr(mean_var[0:S, b], stats[0:S, b]))
                nc.vector.tensor_scalar(rstd[0:S], mean_var[0:S, :, 1], EPS, None, ALU.add).then_inc(s_done, 1)

            def normalize(dst, src, scale, s_ready, s_done):
                dve.wait_ge(s_ready, 1)
                chain(nc.vector.reciprocal(rstd[0:S], std[0:S]))
                if scale != 1.0:
                    chain(nc.vector.tensor_scalar(rstd[0:S], rstd[0:S], scale, None, ALU.mult))
                for b in range(B):
                    nc.vector.tensor_scalar(dst[0:S, b], src[0:S, b], mean_var[0:S, b, 0:1], rstd[0:S, b:b + 1],
                                            ALU.subtract, ALU.mult).then_inc(s_done, 1)

            dve.sem_inc(s_accfree, 1)
            dve.sem_inc(s_yfree, 1)
            dve.wait_ge(s_x, 16)
            moments(x_in, s_var)
            normalize(x_norm, x_in, QSCALE, s_std, s_xnorm)

            def low(n, dst, src, hi):
                dve.wait_ge(s_hi, n + 1)
                nc.vector.tensor_tensor(dst, src, hi, ALU.subtract).then_inc(s_free, 1)

            for u in range(XFILLS):
                cols = slice(u * 2 * S, (u + 1) * 2 * S)
                low(u, xt_lo[:, :, cols], setup_bank[:, u, 0:DC * 2 * S].rearrange("p (c t) -> p c t", c=DC), xt_hi[:, :, cols])
            for which, (hi, lo) in enumerate(((m_hi, m_lo), (n_hi, n_lo))):
                with dve.Fori(0, H // 4) as i:
                    for k in range(4):
                        head = bass.ds(4 * i + k, 1)
                        low(XFILLS + which * H + 4 * i + k, lo[:, head].rearrange("p o c d -> p (o c d)"), setup_bank[:, k, :],
                            hi[:, head].rearrange("p o c d -> p (o c d)"))
            nc.vector.memset(probs[:, :, KV:KPAD], 0.0).then_inc(s_pads, 1)
            dve.wait_ge(s_tanh, 1)

            def route(b, stage_no, j):
                done = [links_before(stage_no)]

                def after(semaphore, count):
                    dve.wait_ge(semaphore, count)
                    dve.sem_inc(s_dseen, 1)

                def link(ins):
                    done[0] += 1
                    ins.then_inc(s_route, 1)
                    after(s_route, b * BATCH_LINKS + done[0])

                if stage_no == 0:
                    if isinstance(b, int) and b == 0:
                        dve.wait_ge(s_zero, 80)
                        dve.wait_ge(s_const, 7)
                    else:
                        after(s_scat, 16 * TOPK * b)
                    after(s_yfree, b + 2)
                    link(nc.vector.bn_stats(stats[0:S, 0], x1_pair[0:S, j]))
                    link(nc.vector.bn_aggr(mean_var[0:S, 0], stats[0:S, 0]))
                    nc.vector.tensor_scalar(std[0:S, 0:1], mean_var[0:S, 0, 1:2], EPS, None, ALU.add).then_inc(s_moments, 1)
                elif stage_no == 1:
                    link(nc.vector.tensor_copy(row[:].bitcast(U32)[0:S, D:D + 1], token_f[0:S]))
                    link(nc.vector.tensor_scalar(token_f[0:S], token_f[0:S], float(S), None, ALU.add))
                    after(s_scale, b + 1)
                    nc.vector.tensor_scalar(row[0:S, 0:D], x1_pair[0:S, j], mean_var[0:S, 0, 0:1], rstd[0:S, 0:1],
                                            ALU.subtract, ALU.mult).then_inc(s_row, 1)
                elif stage_no == 4:
                    after(s_logit, b + 1)
                    nc.vector.tensor_reduce(nmx[0:S], logit_ps[0:S], AX.X, ALU.max, negate=True).then_inc(s_nmx, 1)
                elif stage_no == 6:
                    after(s_ex, b + 1)
                    link(nc.vector.reciprocal(esum[0:S], esum[0:S]))
                    link(nc.vector.tensor_scalar(ex[0:S], ex[0:S], esum[0:S], None, ALU.mult))
                    link(nc.vector.max(top[0:S], ex[0:S]))
                    link(nc.vector.max_index(topi[0:S], top[0:S], ex[0:S]))
                elif stage_no == 7:
                    link(nc.vector.tensor_reduce(wsum[0:S], top[0:S, 0:TOPK], AX.X, ALU.add))
                    link(nc.vector.tensor_scalar(wsum[0:S], wsum[0:S], 1e-20, None, ALU.add))
                    link(nc.vector.reciprocal(wsum[0:S], wsum[0:S]))
                    link(nc.vector.tensor_copy(topf[0:S], topi[0:S, 0:TOPK]))
                    link(nc.vector.tensor_tensor(hot[0:S], iota_e[0:S].unsqueeze(1).to_broadcast([S, TOPK, E]),
                                                 topf[0:S].unsqueeze(2).to_broadcast([S, TOPK, E]), ALU.is_equal))
                elif stage_no == 8:
                    with nc.allow_low_precision("zeros and ones"):
                        link(nc.vector.tensor_reduce(mask[0:S], hot[0:S].rearrange("p k e -> p e k"), AX.X, ALU.add))
                    link(nc.vector.scalar_tensor_tensor(out=row[0:S, D + 1:RW], in0=ex[0:S], scalar=wsum[0:S], in1=mask[0:S],
                                                        op0=ALU.mult, op1=ALU.mult))
                elif stage_no == 10:
                    after(s_pos, b + 1)
                    link(nc.vector.tensor_tensor(hotpos[0:S], hot[0:S], pos_ps[0:S].unsqueeze(1).to_broadcast([S, TOPK, E]), ALU.mult))
                    link(nc.vector.tensor_reduce(pos[0:S], hotpos[0:S], AX.X, ALU.add))
                    link(nc.vector.tensor_tensor(seen[0:S], seen[0:S], mask[0:S], ALU.add))
                elif stage_no == 11:
                    link(nc.vector.tensor_scalar(over[0:S], pos[0:S], float(CAP), None, ALU.is_ge))
                    link(nc.vector.tensor_scalar(pos[0:S], pos[0:S], float(CAP - 1), None, ALU.min))
                    link(nc.vector.scalar_tensor_tensor(out=slot[0:S], in0=topf[0:S], scalar=float(CAP), in1=pos[0:S], op0=ALU.mult, op1=ALU.add))
                    link(nc.vector.tensor_tensor(scat[0:S], dump_row[0:S], slot[0:S], ALU.subtract))
                    link(nc.vector.tensor_tensor(scat[0:S], scat[0:S], over[0:S], ALU.mult))
                    link(nc.vector.tensor_tensor(scat[0:S], scat[0:S], slot[0:S], ALU.add))
                    link(nc.vector.tensor_scalar(dump_row[0:S], dump_row[0:S], float(S * TOPK), None, ALU.add))
                    nc.vector.tensor_copy(scat_u[0:S], scat[0:S]).then_inc(s_slot, 1)
                assert done[0] == links_before(stage_no) + LINKS.get(stage_no, 0)

            def pair(i, first):
                def fill_lo(f):
                    n = FILL[f]
                    src = stage[:, n % 2]
                    if f[0] == "q":
                        _, hp, c = f
                        part = lambda q: q[:, c, :, hp * 2 * S:(hp + 1) * 2 * S].rearrange("p j (h s) -> p j h s", h=2)
                        low(SETUP_FILLS + i * FILLS + n, part(q_lo), src[:, 0:4 * S].rearrange("p (h j s) -> p j h s", h=2, j=2), part(q_hi))
                    else:
                        _, t, k = f
                        m = tile_rows(t)
                        off = 128 * (t % TILES - GROUPS[group_of(t)][0])
                        part = lambda p: p[group_of(t) % 2][0:KP, 4 * k:4 * k + 4, off:off + m]
                        low(SETUP_FILLS + i * FILLS + n, part(pt_lo), src[0:KP, :].rearrange("p (c q) -> p c q", c=4)[:, :, 0:m], part(pt_hi))

                for s in range(ALL_STEPS):
                    for hp, c in Q_FIRST.get(s, []):
                        fill_lo(("q", hp, c))
                    if s < STEPS:
                        m = tile_rows(s)
                        dve.wait_ge(s_scores, i * STEPS + s + 1)
                        nc.vector.tensor_reduce(neg_max[0:m, s % 2:s % 2 + 1], scores[0:m, 0:KV], AX.X, ALU.max, negate=True).then_inc(s_max, 1)
                    fills = fills_of_step(s)
                    for f in fills[:3]:
                        fill_lo(f)
                    if s < STEPS:
                        dve.wait_ge(s_exp, i * STEPS + s + 2)
                        col = slice(s % 2, s % 2 + 1)
                        nc.vector.reciprocal(row_inv[0:m, col], row_sum[0:m, col]).then_inc(s_inv, 1)
                        dve.wait_ge(s_inv, i * STEPS + s + 1)
                        nc.vector.tensor_scalar(probs[0:m, s % 2, 0:KV], probs[0:m, s % 2, 0:KV], row_inv[0:m, col], PSCALE,
                                                ALU.mult, ALU.mult).then_inc(s_norm, 1)
                    for f in fills[3:]:
                        fill_lo(f)
                    if s in PV and PV[s][3] == KC:
                        j, g, _, _ = PV[s]
                        w = group_width(g)
                        for c in range(DC):
                            dve.wait_ge(s_uhi, i * 2 * NG * DC + (j * NG + g) * DC + c + 1)
                            cols = slice(g * 256, g * 256 + w)
                            nc.vector.scalar_tensor_tensor(out=ut_lo[:, c, cols], in0=acc[:, c, 0:w], scalar=1.0 / PSCALE, in1=ut_hi[:, c, cols],
                                                           op0=ALU.mult, op1=ALU.subtract).then_inc(s_accfree, 1)
                    if s in Y_STEP:
                        j = Y_STEP[s]
                        dve.wait_ge(s_yfull, 2 * i + j + 1)
                        dve.wait_ge(s_xin[j], 16 * (i + 1))
                        nc.vector.scalar_tensor_tensor(out=x1_pair[0:S, j], in0=yps[0:S, 0:D], scalar=gates[0:S, 2:3], in1=x1_pair[0:S, j],
                                                       op0=ALU.mult, op1=ALU.add).then_inc(s_yfree, 1)
                    for j, stage_no in routing_at(s, first):
                        route(2 * i + j, stage_no, j % 2)

            pair(0, True)
            with dve.Fori(1, PAIRS) as i:
                pair(i, False)

            def up_low(e, k):
                dve.wait_ge(s_guhi, e + 1)
                nc.vector.tensor_tensor(wgu_lo[:, k], wgu[:, k], wgu_hi[:, k], ALU.subtract).then_inc(s_gulo, 1)

            def down_low(e, k):
                dve.wait_ge(s_wdhi, e + 1)
                nc.vector.tensor_tensor(wd_lo[:, k], wd[:, k], wd_hi[:, k], ALU.subtract).then_inc(s_wlo, 1)

            def shared_hidden(u):
                fc, half = u // 2, u % 2
                dve.wait_ge(s_shact, u + 1)
                nc.vector.tensor_tensor(sh_h[:, fc, half * (NTOK // 2):(half + 1) * (NTOK // 2)], sh_act[:, u % 2],
                                        acc[0:FP, u % 2, 0:NTOK // 2], ALU.mult).then_inc(s_shh, 1)

            for stage_no in (0, 1, 4):
                route(B - 1, stage_no, 1)
            shared_hidden(0)
            for stage_no in (6, 7, 8):
                route(B - 1, stage_no, 1)
            shared_hidden(1)
            for stage_no in (10, 11):
                route(B - 1, stage_no, 1)
            for u in range(2, 2 * FSC):
                shared_hidden(u)
            dve.wait_ge(s_res, 16)
            for b in range(B):
                dve.wait_ge(s_shdown, b + 1)
                nc.vector.scalar_tensor_tensor(out=x1[0:S, b], in0=stage[0:S, b % 2, 0:D], scalar=gates[0:S, 3:4],
                                               in1=x1[0:S, b], op0=ALU.mult, op1=ALU.add).then_inc(s_shout, 1)
            def rows_low(e, k2):
                dve.wait_ge(s_xhi, e + 1)
                nc.vector.tensor_tensor(xet_lo[:, k2], stage[:, k2, 0:DC * CAP].rearrange("p (c t) -> p c t", c=DC), xet_hi[:, k2],
                                        ALU.subtract).then_inc(s_xlo, 1)

            def hidden(e, k2):
                dve.wait_ge(s_act, e + 1)
                nc.vector.tensor_tensor(hid[:, k2], act[:, k2], acc[0:FP, k2, 0:FC * CAP].rearrange("p (c t) -> p c t", c=FC),
                                        ALU.mult).then_inc(s_hid, 1)

            def hidden_low(e, k2):
                dve.wait_ge(s_hhi, e + 1)
                nc.vector.tensor_tensor(hid_lo[:, k2], hid[:, k2], hid_hi[:, k2], ALU.subtract).then_inc(s_hlo, 1)

            def turn(i, first, last):
                for k in range(UN):
                    e, k2 = UN * i + k, k % 2
                    if not (last and k == UN - 1):
                        rows_low(e + 1, (k + 1) % 2)
                    if not (last and k >= UN - 2):
                        up_low(e + 2, (k + 2) % NW)
                    hidden(e, k2)
                    if not (last and k >= UN - 2):
                        down_low(e + 2, (k + 2) % NW)
                    hidden_low(e, k2)

            for e in range(2):
                up_low(e, e)
                down_low(e, e)
            rows_low(0, 0)
            turn(0, True, False)
            with dve.Fori(1, E // UN - 1) as i:
                turn(i, False, False)
            turn(E // UN - 1, False, True)
            for half in range(2):
                bs = slice(half * (B // 2), (half + 1) * (B // 2))
                dve.wait_ge(s_back[half], 32)
                chain(nc.vector.tensor_tensor(back[0:S, 0, bs], back[0:S, 0, bs], back[0:S, 1, bs], ALU.add))
                nc.vector.scalar_tensor_tensor(out=result[0:S, bs], in0=back[0:S, 0, bs], scalar=gates[0:S, 3:4], in1=x1[0:S, bs],
                                               op0=ALU.mult, op1=ALU.add).then_inc(s_fin, 1)

        @block.tensor
        def _(pe):
            def take(n):
                pe.wait_ge(s_free, n - 1)

            def products(dst, pairs, first=True, last=True):
                steps = [(l, r) for lh, ll, rh, rl in pairs for l, r in ((lh, rh), (lh, rl), (ll, rh))]
                for n, (l, r) in enumerate(steps):
                    ins = nc.tensor.matmul(dst, l, r, start=first and n == 0, stop=last and n == len(steps) - 1)
                return ins

            def transposes(src, n, bank, s_done):
                for c in range(DC):
                    for j in range(2):
                        col = (c * 2 + j) * S
                        ins = nc.tensor.transpose(bank[:, col:col + S], src[0:S, 2 * n + j, c * 128:(c + 1) * 128], ident[0:S, 0:S])
                ins.then_inc(s_done, 1)

            pe.wait_ge(s_ident, 1)
            for u in range(XFILLS):
                pe.wait_ge(s_xnorm, 2 * u + 2)
                transposes(x_norm, u, setup_bank[:, u], s_full)
            for which in range(2):
                with pe.Fori(0, QUADS // 2) as i:
                    for k in range(2):
                        pe.wait_ge(s_w[k], 32 * (which * 2 + i + 1))
                        for h in range(4):
                            n = XFILLS + which * H + (2 * i + k) * 4 + h
                            pe.wait_ge(s_free, n - 3)
                            for c in range(DC):
                                ins = nc.tensor.matmul(setup_bank[:, h, c * D:(c + 1) * D], w_raw[:, k, 0, h, c * 128:(c + 1) * 128],
                                                       w_raw[:, k, 1, h, :], start=True, stop=True)
                            if h == 3:
                                ins.then_inc(s_full, 1)
                                nc.tensor.transpose(yps[:, 0:128], ident[:], ident[:]).then_inc(s_wused, 1)
                            else:
                                ins.then_inc(s_full, 1)
            pe.wait_ge(s_pads, 1)

            def route(b, stage_no, rows=row_t):
                if stage_no == 2:
                    if not (isinstance(b, int) and b == 0):
                        pe.wait_ge(s_slot, b)
                    pe.wait_ge(s_row, b + 1)
                    for c in range(DC):
                        ins = nc.tensor.transpose(row_ps[:, c * S:(c + 1) * S], row[0:S, c * 128:(c + 1) * 128], ident[0:S, 0:S])
                    ins.then_inc(s_rowps, 1)
                elif stage_no == 3:
                    pe.wait_ge(s_gw, 16)
                    pe.wait_ge(s_rowt, b + 1)
                    for c in range(DC):
                        ins = nc.tensor.matmul(logit_ps[0:S], rows[:, c], gate_w[:, c, :], start=c == 0, stop=c == DC - 1)
                    ins.then_inc(s_logit, 1)
                elif stage_no == 9:
                    pe.wait_ge(s_route, b * BATCH_LINKS + links_before(9))
                    nc.tensor.matmul(pos_ps[0:S], ones[0:S, :], seen[0:S], start=True, stop=False)
                    nc.tensor.matmul(pos_ps[0:S], tri[0:S, :], mask[0:S], start=False, stop=True).then_inc(s_pos, 1)

            def pair(i, first):
                def q_fill(hp, c):
                    n = FILL[("q", hp, c)]
                    take(SETUP_FILLS + i * FILLS + n)
                    for h in range(2):
                        dst = stage[:, n % 2, h * 2 * S:(h + 1) * 2 * S]
                        cols = slice(c * 128, (c + 1) * 128)
                        ins = products(dst, [(m_hi[:, 2 * hp + h, k, cols], m_lo[:, 2 * hp + h, k, cols],
                                              xt_hi[:, k, bass.ds(i * 2 * S, 2 * S)], xt_lo[:, k, bass.ds(i * 2 * S, 2 * S)]) for k in range(DC)])
                    ins.then_inc(s_full, 1)

                def t_fill(t, k):
                    n = FILL[("T", t, k)]
                    if k == 0:
                        pe.wait_ge(s_norm, i * STEPS + t + 1)
                    take(SETUP_FILLS + i * FILLS + n)
                    for c in range(4):
                        ins = nc.tensor.transpose(stage[0:KP, n % 2, c * 128:(c + 1) * 128],
                                                  probs[:, t % 2, (4 * k + c) * KP:(4 * k + c + 1) * KP], ident[:])
                    ins.then_inc(s_full, 1)

                def weighted_sum(j, g, c0, c1):
                    w = group_width(g)
                    if c0 == 0:
                        pe.wait_ge(s_accfree, i * 2 * NG * DC + (j * NG + g) * DC + 1)
                        pe.wait_ge(s_free, SETUP_FILLS + i * FILLS + FILL[("T", j * TILES + GROUPS[g][-1], TBANKS - 1)] + 1)
                        if g == 0:
                            pe.wait_ge(s_split, (2 * i + j + 1) * PIECES)
                    for c in range(c0, c1):
                        for d in range(DC):
                            cols = slice(d * 128, (d + 1) * 128)
                            ins = products(acc[:, d, 0:w], [(c_hi[0:KP, j, c, cols], c_lo[0:KP, j, c, cols],
                                                             pt_hi[g % 2][0:KP, c, 0:w], pt_lo[g % 2][0:KP, c, 0:w])],
                                           first=c == 0, last=c == KC - 1)
                            if c == KC - 1:
                                ins.then_inc(s_accfull, 1)

                for s in range(ALL_STEPS):
                    for hp, c in Q_FIRST.get(s, []):
                        q_fill(hp, c)
                    if s < STEPS:
                        j, t = divmod(s, TILES)
                        m = tile_rows(s)
                        if t == 0:
                            pe.wait_ge(s_split, (2 * i + j) * PIECES + 4)
                        if s < 6:
                            pe.wait_ge(s_free, SETUP_FILLS + i * FILLS + FILL[("q", min(((s + 1) * 128 - 1) // (2 * S), H // 2 - 1), DC - 1)] + 1)
                        elif s == 6:
                            pe.wait_ge(s_free, SETUP_FILLS + i * FILLS + FILL[("q", H // 2 - 1, DC - 1)] + 1)
                        pe.wait_ge(s_exp, i * STEPS + s + 1)
                        rows = slice(t * 128, t * 128 + m)
                        for k0 in range(0, KV, 512):
                            k1 = min(k0 + 512, KV)
                            ins = products(scores[0:m, k0:k1], [(q_hi[:, c, j, rows], q_lo[:, c, j, rows],
                                                                 ct_hi[:, j, c, k0:k1], ct_lo[:, j, c, k0:k1]) for c in range(DC)])
                        ins.then_inc(s_scores, 1)
                    fills = fills_of_step(s)
                    for f in fills[:2]:
                        (q_fill if f[0] == "q" else t_fill)(*f[1:])
                    piece = PV.get(s)
                    if s == 27:
                        piece = None
                    if piece:
                        j, g, c0, c1 = piece
                        mid = (c0 + c1) // 2
                        weighted_sum(j, g, c0, mid)
                    for f in fills[2:]:
                        (q_fill if f[0] == "q" else t_fill)(*f[1:])
                    if s == 27:
                        j, g, c0, mid = PV[27][0], PV[27][1], PV[27][2], PV[27][2]
                        piece = PV[27]
                    if piece:
                        weighted_sum(j, g, mid, piece[3])
                    if s in Y_STEP:
                        j = Y_STEP[s]
                        pe.wait_ge(s_accfree, i * 2 * NG * DC + (j + 1) * NG * DC + 1)
                        pe.wait_ge(s_yfree, 2 * i + j + 1)
                        ins = products(yps[0:S, 0:D], [(ut_hi[:, c, h * S:(h + 1) * S], ut_lo[:, c, h * S:(h + 1) * S],
                                                        n_hi[:, h, c, :], n_lo[:, h, c, :]) for h in range(H) for c in range(DC)])
                        ins.then_inc(s_yfull, 1)
                    for j, stage_no in routing_at(s, first):
                        route(2 * i + j, stage_no)

            pair(0, True)
            with pe.Fori(1, PAIRS) as i:
                pair(i, False)

            def shared_up(u):
                fc, half = u // 2, u % 2
                toks = slice(half * (NTOK // 2), (half + 1) * (NTOK // 2))
                if u >= 2:
                    pe.wait_ge(s_shh, u - 1)
                for dst, w in ((ps[0:FP, u % 2], shg), (acc[0:FP, u % 2], shu)):
                    for c in range(DC):
                        ins = nc.tensor.matmul(dst[:, 0:NTOK // 2], w[:, c, fc * FP:(fc + 1) * FP], xnt[:, c, toks], start=c == 0, stop=c == DC - 1)
                ins.then_inc(s_shup, 1)

            route(B - 1, 2)
            route(B - 1, 3, xnt[:, :, (B - 1) * S:NTOK])
            pe.wait_ge(s_fw, 48)
            pe.wait_ge(s_xnt, 16)
            for u in range(2):
                shared_up(u)
            route(B - 1, 9)
            for u in range(2, 2 * FSC):
                shared_up(u)
            pe.wait_ge(s_shh, 2 * FSC)
            for b in range(B):
                if b >= 2:
                    pe.wait_ge(s_shout, b - 1)
                for fc in range(FSC):
                    ins = nc.tensor.matmul(stage[0:S, b % 2, 0:D], sh_h[:, fc, b * S:(b + 1) * S], shd[:, fc, :], start=fc == 0, stop=fc == FSC - 1)
                ins.then_inc(s_shdown, 1)
            pe.wait_ge(s_shout, B)

            def rows_in(e, k, guard, loads):
                pe.wait_ge(s_xe[k], loads)
                if guard:
                    pe.wait_ge(s_xlo, e - 1)
                for c in range(DC):
                    for h in range(SC):
                        ins = nc.tensor.transpose(stage[:, k % 2, c * CAP + h * SP_:c * CAP + (h + 1) * SP_],
                                                  xe[:, k, h, c * 128:(c + 1) * 128], ident[0:SP_, 0:SP_])
                ins.then_inc(s_xt, 1)

            def up(e, k, guard):
                pe.wait_ge(s_wlo, e + 1)
                pe.wait_ge(s_xlo, e + 1)
                if guard:
                    pe.wait_ge(s_hid, e - 1)
                k2 = k % 2
                for which, dst in enumerate((ps[0:FP, k2], acc[0:FP, k2])):
                    for fc in range(FC):
                        cols = slice(which * F + fc * FP, which * F + (fc + 1) * FP)
                        ins = products(dst[:, fc * CAP:(fc + 1) * CAP], [(wgu_hi[:, k, c, cols], wgu_lo[:, k, c, cols],
                                                                          xet_hi[:, k2, c], xet_lo[:, k2, c]) for c in range(DC)])
                ins.then_inc(s_up, 1)

            def down(e, k, guard):
                pe.wait_ge(s_hlo, e + 1)
                if guard:
                    pe.wait_ge(s_eo, e - 1)
                k2 = k % 2
                dst = (ps[0:SP_, 2], yps[0:SP_])[k2]
                for h in range(SC):
                    slots = slice(h * SP_, (h + 1) * SP_)
                    ins = products(dst[:, h * D:(h + 1) * D], [(hid_hi[:, k2, fc, slots], hid_lo[:, k2, fc, slots],
                                                                wd_hi[:, k, fc], wd_lo[:, k, fc]) for fc in range(FC)])
                ins.then_inc(s_down, 1)

            def turn(i, first, last):
                for k in range(UN):
                    e = UN * i + k
                    if not (last and k == UN - 1):
                        rows_in(e + 1, (k + 1) % UN, not (first and k == 0), 32 * (i + 1 + (k + 1) // UN))
                    up(e, k % NW, not (first and k < 2))
                    if not (first and k == 0):
                        down(e - 1, (k - 1) % NW, not (first and k < 3))

            rows_in(0, 0, False, 32)
            turn(0, True, False)
            with pe.Fori(1, E // UN - 1) as i:
                turn(i, False, False)
            turn(E // UN - 1, False, True)
            down(E - 1, NW - 1, True)


def kernel(**inputs):
    import numpy as _np
    import concourse.bacc as _bacc
    from concourse import mybir as _mybir
    from concourse.bass_utils import run_bass_kernel_spmd as _run

    a = {k: _np.asarray(v) for k, v in inputs.items()}

    def chunks(w, p):
        e, r, c = w.shape
        return w.reshape(e, r // p, p, c).transpose(0, 2, 1, 3)

    ins = {
        "x": a["x"],
        "ctx_rows": a["ctx_2048"],
        "ctx_cols": a["ctx_2048"].transpose(0, 2, 1),
        "wq_t": a["L0_xattn_Wq"].T,
        "wk_t": a["L0_xattn_Wk"].T,
        "wv_t": a["L0_xattn_Wv"].T,
        "wo": a["L0_xattn_Wo"],
        "g_xattn": a["g_xattn"],
        "g_ffn": a["g_ffn"],
        "gate_t": a["L0_ffn_gate_w"].T,
        "egu_t": chunks(_np.concatenate([a["L0_ffn_w_gate"], a["L0_ffn_w_up"]], axis=1).transpose(0, 2, 1), 128),
        "ed_t": chunks(a["L0_ffn_w_down"].transpose(0, 2, 1), 88),
        "sg_t": a["L0_ffn_sh_gate"].T,
        "su_t": a["L0_ffn_sh_up"].T,
        "sd_t": a["L0_ffn_sh_down"].T,
    }
    nc = _bacc.Bacc("TRN2", target_bir_lowering=False, num_devices=1)
    arrays, args = {}, []
    for name, v in ins.items():
        v = _np.ascontiguousarray(v)
        arrays[f"in_{name}"] = v
        args.append(nc.dram_tensor(f"in_{name}", v.shape, _mybir.dt.from_np(v.dtype), kind="ExternalInput").ap())
    args.append(nc.dram_tensor("out_y", (8, 100, 256), _mybir.dt.float32, kind="ExternalOutput").ap())
    gated_cross_attention_moe(nc, *args)
    r = _run(nc, [arrays], core_ids=[0])
    return r.results[0]["out_y"]
```

```python
from contextlib import ExitStack

import concourse.bass as bass
from concourse import mybir

ALU = mybir.AluOpType
ACT = mybir.ActivationFunctionType
AX = mybir.AxisListType
F32 = mybir.dt.float32
F16 = mybir.dt.float16
BF16 = mybir.dt.bfloat16
U32 = mybir.dt.uint32

B, S, D = 8, 100, 256
H, HD = 16, 128
KV = 1444
DC = D // 128
KC = 12
KP = -(-KV // KC)
KLAST = KV - (KC - 1) * KP
KPAD = KC * KP
Q = H * S
TILES = -(-Q // 128)
TLAST = Q - (TILES - 1) * 128
PAIRS = B // 2
EPS = 1e-5
QSCALE = float(HD) ** -0.5
PSCALE = 16384.0
F16MAX = 65504.0

E, F, FS, TOPK = 64, 176, 352, 6
NTOK = B * S
CAP = 2 * -(-NTOK * TOPK // E)
SC = 2
SP_ = CAP // SC
FP = 88
FC = F // FP
FSC = FS // FP
SHARED_UP = (5, 6, 4)
SHARED_DOWN = (7, 2)
DUMP = E * CAP
SUMP = 95
assert (NTOK + CAP) % SUMP == 0 and DUMP == 128 * SP_
RW = D + 1 + E
UN = 8

STEPS = 2 * TILES
GROUPS = [(0, 1), (2, 3), (4, 5), (6, 7), (8, 9), (10, 11, 12)]
NG = len(GROUPS)


def tile_rows(t):
    return TLAST if t % TILES == TILES - 1 else 128


def group_of(t):
    return min((t % TILES) // 2, NG - 1)


def group_width(g):
    return sum(tile_rows(t) for t in GROUPS[g])


AHEAD = 3
Q_AFTER = {n: AHEAD + n for n in range(H // 2 - AHEAD)}
AHEAD_EARLY = {27: [(1, 1)]}
AHEAD_LATE = {25: [(0, 0)], 26: [(0, 1), (1, 0)], 28: [(2, 0), (2, 1)]}
TBANKS = KC // 4


def t_fills(s):
    return [("T", s - 1, k) for k in range(TBANKS)] if 1 <= s <= STEPS else []


def q_fills(s):
    return [("q", Q_AFTER[s], c) for c in range(DC)] if s in Q_AFTER else []


def ahead_fills(s, late):
    return [("ahead", hp, c) for hp, c in (AHEAD_LATE if late else AHEAD_EARLY).get(s, [])]


FILL = {}
for _s in range(STEPS + 3):
    for _f in t_fills(_s) + q_fills(_s) + ahead_fills(_s, False) + ahead_fills(_s, True):
        FILL[_f] = len(FILL)
FILLS = len(FILL)
N_AT = {3 + n // 2: [n - n % 2, n - n % 2 + 1] for n in range(H)}


def n_fills(s, first):
    return [("N", h, 0) for h in N_AT.get(s, [])] if first else []


FIRST_FILL = {}
for _s in range(STEPS + 3):
    for _f in t_fills(_s) + q_fills(_s) + n_fills(_s, True) + ahead_fills(_s, False) + ahead_fills(_s, True):
        FIRST_FILL[_f] = len(FIRST_FILL)
assert len(FIRST_FILL) == FILLS + H and H % 2 == 0
LAST_FILL = {}
for _s in range(STEPS + 3):
    for _f in t_fills(_s) + q_fills(_s):
        LAST_FILL[_f] = len(LAST_FILL)
assert FILLS % 2 == 0 and FILLS == H // 2 * DC + TBANKS * STEPS


PV = {}
for _j in range(2):
    _o = _j * TILES
    for _g in range(4):
        PV[_o + 2 * _g + 3] = (_j, _g, 0, 6)
        PV[_o + 2 * _g + 4] = (_j, _g, 6, 12)
    for _n in range(3):
        PV[_o + 11 + _n] = (_j, 4, 4 * _n, 4 * _n + 4)
    PV[_o + 14] = (_j, 5, 0, 6)
    PV[_o + 15] = (_j, 5, 6, 12)
Y_STEP = {16: 0, 28: 1}
ALL_STEPS = STEPS + 3
ROUTE_AT = {0: 16, 1: 1}
ROUTE_STAGES = 12
LINKS = {0: 2, 1: 2, 6: 4, 7: 5, 8: 2, 10: 5, 11: 7}
BATCH_LINKS = sum(LINKS.values())


def links_before(stage):
    return sum(n for at, n in LINKS.items() if at < stage)


def routing_at(step, first):
    out = []
    for j, start in ROUTE_AT.items():
        if 0 <= step - start < ROUTE_STAGES and not (j == 1 and first):
            out.append((-1 if j == 1 else 0, step - start))
    return out



XFILLS = PAIRS
assert XFILLS == 4 and H % 4 == 0
SETUP_FILLS = H + XFILLS
FIRST_FILLS = SETUP_FILLS + AHEAD * DC
LATER_FILLS = FIRST_FILLS + len(FIRST_FILL) - FILLS
assert SETUP_FILLS % 2 == 0 and AHEAD * DC % 2 == 0


def fill_number(f, i, first, last):
    if first:
        return FIRST_FILLS + FIRST_FILL[f], FIRST_FILL[f] % 2
    at = (LAST_FILL if last else FILL)[f]
    return LATER_FILLS + i * FILLS + at, at % 2


QUADS = H // 4
PIECES = 10


def gated_cross_attention_moe(nc, x, ctx_rows, ctx_cols, wq_t, wk_t, wv_t, wo, g_xattn, g_ffn, gate_t,
                              egu_t, ed_t, sg_t, su_t, sd_t, out):
    xn_rows = nc.dram_tensor("xn_rows", [DUMP + NTOK * TOPK, RW], F32, kind="Internal").ap()
    moe_sum = [nc.dram_tensor(f"moe_sum{n}", [NTOK + CAP, D], F32, kind="Internal").ap() for n in range(2)]
    x1_rows = nc.dram_tensor("x1_rows", [B, S, D], F32, kind="Internal").ap()
    xnt_cols = nc.dram_tensor("xnt_cols", [128, DC, NTOK], F32, kind="Internal").ap()

    stack = ExitStack()
    with stack:
        def sb(where, name, shape, dt=F32):
            return where.enter_context(nc.sbuf_tensor(name, shape, dt))

        def sem(name):
            return stack.enter_context(nc.semaphore(name))

        ps = stack.enter_context(nc.psum_tensor("ps", [128, 8, 512], F32))
        scores = ps[:, 0:3, :].rearrange("p a n -> p (a n)")
        stage = ps[:, 3:5, :]
        setup_bank = ps[:, 3:7, :]
        acc = ps[:, 5:7, :]
        yps = ps[:, 7, :]
        row_ps = yps[:, D:D + DC * S]
        logit_ps = yps[:, D:D + E]
        pos_ps = yps[:, D + 2 * E:D + 3 * E]

        ident = sb(stack, "ident", [128, 128])
        gates = sb(stack, "gates", [128, 4])
        stats = sb(stack, "stats", [128, B, 6])
        mean_var = sb(stack, "mean_var", [128, B, 2])
        rstd = sb(stack, "rstd", [128, B])
        std = sb(stack, "std", [128, B])
        x1_pair = sb(stack, "x1_pair", [128, 2, D])
        row = sb(stack, "row", [128, 2, RW])
        gate_w = sb(stack, "gate_w", [128, DC, E])
        ex = sb(stack, "ex", [128, E])
        nmx = sb(stack, "nmx", [128, 1])
        esum = sb(stack, "esum", [128, 1])
        top = sb(stack, "top", [128, 8])
        topi = sb(stack, "topi", [128, 8], U32)
        topf = sb(stack, "topf", [128, TOPK])
        wsum = sb(stack, "wsum", [128, 1])
        hot = sb(stack, "hot", [128, TOPK, E], BF16)
        KS = 4
        hotpos = sb(stack, "hotpos", [128, KS, E])
        row_t = hotpos[:].rearrange("p k e -> p (k e)")[:, 0:DC * S].rearrange("p (c t) -> p c t", c=DC)
        empty = hotpos[:].rearrange("p k e -> p (k e)").bitcast(U32)[0:E, 0:CAP]
        mask = sb(stack, "mask", [128, E], BF16)
        seen = sb(stack, "seen", [128, E], BF16)
        ones = sb(stack, "ones", [128, S], BF16)
        tri = sb(stack, "tri", [128, S], BF16)
        iota_e = sb(stack, "iota_e", [128, E])
        dump_row = sb(stack, "dump_row", [128, TOPK])
        minus_half = sb(stack, "minus_half", [128, 1])
        token_f = sb(stack, "token_f", [128, 1])
        pos = sb(stack, "pos", [128, TOPK])
        over = sb(stack, "over", [128, TOPK])
        slot = sb(stack, "slot", [128, TOPK])
        scat = sb(stack, "scat", [128, TOPK])
        scat_u = sb(stack, "scat_u", [128, 2, TOPK], U32)

        attn = ExitStack()
        xt_hi = sb(attn, "xt_hi", [128, DC, NTOK], F16)
        xt_lo = sb(attn, "xt_lo", [128, DC, NTOK], BF16)
        m_hi = sb(attn, "m_hi", [128, H, DC, D], F16)
        m_lo = sb(attn, "m_lo", [128, H, DC, D], BF16)
        n_hi = sb(attn, "n_hi", [128, H, DC, D], F16)
        n_lo = sb(attn, "n_lo", [128, H, DC, D], BF16)
        q_hi = sb(attn, "q_hi", [128, DC, 2, Q], F16)
        q_lo = sb(attn, "q_lo", [128, DC, 2, Q], BF16)
        ct_hi = sb(attn, "ct_hi", [128, 2, DC, KV], F16)
        ct_lo = sb(attn, "ct_lo", [128, 2, DC, KV], BF16)
        c_hi = sb(attn, "c_hi", [128, 2, KC, D], F16)
        c_lo = sb(attn, "c_lo", [128, 2, KC, D], BF16)
        raw = sb(attn, "raw", [128, 2, KV // 2])
        neg_max = sb(attn, "neg_max", [128, 2])
        part_max = sb(attn, "part_max", [128, 2])
        row_sum = sb(attn, "row_sum", [128, 2])
        row_inv = sb(attn, "row_inv", [128, 2])
        setup = ExitStack()
        x_in = sb(setup, "x_in", [128, B, D])
        x_norm = sb(setup, "x_norm", [128, B, D])
        w_raw = sb(setup, "w_raw", [128, 2, 2, 4, D])
        setup.close()
        wv_raw = n_hi[:].bitcast(F32).rearrange("p h c d -> p h (c d)")
        wo_raw = n_lo[:].bitcast(F32).rearrange("p h c d -> p h (c d)")
        probs = sb(attn, "probs", [128, 2, KPAD])
        pt_hi = [sb(attn, f"pt_hi{n}", [128, KC, group_width(4 + n)], F16) for n in range(2)]
        pt_lo = [sb(attn, f"pt_lo{n}", [128, KC, group_width(4 + n)], BF16) for n in range(2)]
        ut_hi = sb(attn, "ut_hi", [128, DC, Q], F16)
        ut_lo = sb(attn, "ut_lo", [128, DC, Q], BF16)
        attn.close()

        ffn = ExitStack()
        xnt = sb(ffn, "xnt", [128, DC, NTOK])
        xnt_hi = sb(ffn, "xnt_hi", [128, DC, NTOK], F16)
        xnt_lo = sb(ffn, "xnt_lo", [128, DC, NTOK], BF16)
        sgu = sb(ffn, "sgu", [128, 2, DC, FS])
        sgu_hi = sb(ffn, "sgu_hi", [128, 2, DC, FS], F16)
        sgu_lo = sb(ffn, "sgu_lo", [128, 2, DC, FS], BF16)
        shd = sb(ffn, "shd", [FP, FSC, D])
        assert 8 * DC * NTOK + 16 * DC * FS + 4 * FSC * D <= 4 * DC * NTOK + 4 * H * DC * D
        x1 = sb(ffn, "x1", [128, B, D])
        result = sb(ffn, "result", [128, B, D])
        sh_act = sb(ffn, "sh_act", [FP, 3, NTOK // 2])
        sh_h = sb(ffn, "sh_h", [FP, FSC, NTOK])
        NW = 4
        wgu = sb(ffn, "wgu", [128, NW, DC, 2 * F])
        wgu_hi = sb(ffn, "wgu_hi", [128, NW, DC, 2 * F], F16)
        wgu_lo = sb(ffn, "wgu_lo", [128, NW, DC, 2 * F], BF16)
        wd = sb(ffn, "wd", [FP, NW, FC, D])
        wd_hi = sb(ffn, "wd_hi", [FP, NW, FC, D], F16)
        wd_lo = sb(ffn, "wd_lo", [FP, NW, FC, D], BF16)
        xe = sb(ffn, "xe", [SP_, UN, SC, D + 1 + UN])
        xet_hi = sb(ffn, "xet_hi", [128, 2, DC, CAP], F16)
        xet_lo = sb(ffn, "xet_lo", [128, 2, DC, CAP], BF16)
        act = sb(ffn, "act", [FP, 2, FC, CAP])
        hid = sb(ffn, "hid", [FP, 2, FC, CAP])
        hid_hi = sb(ffn, "hid_hi", [FP, 2, FC, CAP], F16)
        hid_lo = sb(ffn, "hid_lo", [FP, 2, FC, CAP], BF16)
        eo = sb(ffn, "eo", [SP_, 2, SC, D])
        back = sb(ffn, "back", [128, 2, B, D])
        ffn.close()

        s_x, s_g, s_ident = sem("s_x"), sem("s_g"), sem("s_ident")
        s_dve, s_pool = sem("s_dve"), sem("s_pool")
        s_var, s_std, s_xnorm, s_tanh = sem("s_var"), sem("s_std"), sem("s_xnorm"), sem("s_tanh")
        s_w = [sem(f"s_w{n}") for n in range(QUADS)]
        s_wused, s_wn = sem("s_wused"), sem("s_wn")
        s_full, s_hi, s_free = sem("s_full"), sem("s_hi"), sem("s_free")
        s_twobanks, s_part = sem("s_twobanks"), sem("s_part")
        s_scores, s_max, s_exp, s_inv, s_norm = (sem(n) for n in ("s_scores", "s_max", "s_exp", "s_inv", "s_norm"))
        s_accfull, s_uhi, s_accfree = sem("s_accfull"), sem("s_uhi"), sem("s_accfree")
        s_yfull, s_yfree = sem("s_yfull"), sem("s_yfree")
        s_yst = [sem("s_yst0"), sem("s_yst1")]
        s_raw = [sem("s_raw0"), sem("s_raw1")]
        s_split = sem("s_split")
        s_pads, s_seen = sem("s_pads"), sem("s_seen")
        s_z, s_zero = sem("s_z"), sem("s_zero")
        s_xin = [sem("s_xin0"), sem("s_xin1")]
        s_res, s_gw, s_fw, s_xnt = sem("s_res"), sem("s_gw"), sem("s_fw"), sem("s_xnt")
        s_row, s_rowps, s_rowt, s_rowst = sem("s_row"), sem("s_rowps"), sem("s_rowt"), sem("s_rowst")
        s_logit, s_nmx, s_ex, s_pos, s_slot, s_scat = (sem(n) for n in ("s_logit", "s_nmx", "s_ex", "s_pos", "s_slot", "s_scat"))
        s_shsplit, s_lasthi = sem("s_shsplit"), sem("s_lasthi")
        s_moments, s_scale = sem("s_moments"), sem("s_scale")
        s_route = sem("s_route")
        s_dseen, s_lseen, s_pseen = sem("s_dseen"), sem("s_lseen"), sem("s_pseen")
        s_const = sem("s_const")
        s_shup, s_shact, s_shh, s_shdown, s_shout = (sem(n) for n in ("s_shup", "s_shact", "s_shh", "s_shdown", "s_shout"))
        s_we = [sem(f"s_we{n}") for n in range(4)]
        s_xe = [sem(f"s_xe{n}") for n in range(UN)]
        s_guhi, s_wdhi, s_gulo, s_wlo = sem("s_guhi"), sem("s_wdhi"), sem("s_gulo"), sem("s_wlo")
        s_xt, s_xhi, s_xlo = sem("s_xt"), sem("s_xhi"), sem("s_xlo")
        s_up, s_act, s_hid, s_hhi, s_hlo, s_down, s_eo = (sem(n) for n in ("s_up", "s_act", "s_hid", "s_hhi", "s_hlo", "s_down", "s_eo"))
        s_add = [sem("s_add0"), sem("s_add1")]
        s_back = [sem("s_back0"), sem("s_back1")]
        s_out, s_fin = sem("s_out"), sem("s_fin")

        def m_factors(n):
            if n < 2:
                return w_raw[:, n, 0], w_raw[:, n, 1]
            return wv_raw[:, 4 * n:4 * n + 4], wo_raw[:, 4 * n:4 * n + 4]

        xr = x.rearrange("b s d -> s b d")
        heads4 = lambda w, n: w[bass.ds(n * 4 * HD, 4 * HD), :].rearrange("(h p) d -> p h d", p=HD)

        block = stack.enter_context(nc.Block())

        @block.sync
        def _(sp):
            sp.dma_start(x_in[0:S, :, :], xr).then_inc(s_x, 16)
            sp.dma_start(gates[:, 0:1], g_xattn.partition_broadcast(128)).then_inc(s_g, 16)
            sp.dma_start(gates[:, 1:2], g_ffn.partition_broadcast(128)).then_inc(s_g, 16)

            def weights(n):
                for dst, w in zip(m_factors(n), (wq_t, wk_t)):
                    sp.dma_start(dst, heads4(w, n)).then_inc(s_w[n], 16)

            def context(n, fresh, pieces=range(PIECES)):
                for k in pieces:
                    if not (fresh and k < 2):
                        sp.wait_ge(s_split, n * PIECES + k - 1)
                    dst = raw[:, k % 2]
                    if k < 4:
                        c, half = k // 2, k % 2
                        sp.dma_start(dst, ctx_cols[bass.ds(n, 1), c * 128:(c + 1) * 128, half * (KV // 2):(half + 1) * (KV // 2)]
                                     .rearrange("o p n -> (o p) n")).then_inc(s_raw[k % 2], 16)
                    else:
                        c = 2 * (k - 4)
                        dst = dst[:, 0:2 * D].rearrange("p (c d) -> p c d", c=2)
                        src = ctx_rows[bass.ds(n, 1), :, :].rearrange("o n d -> (o n) d")
                        if c + 2 < KC:
                            sp.dma_start(dst[0:KP], src[c * KP:(c + 2) * KP, :].rearrange("(c p) d -> p c d", p=KP)).then_inc(s_raw[k % 2], 16)
                        else:
                            sp.dma_start(dst[0:KP, 0], src[c * KP:(c + 1) * KP, :]).then_inc(s_raw[k % 2], 16)
                            sp.dma_start(dst[0:KLAST, 1], src[(c + 1) * KP:KV, :]).then_inc(s_raw[k % 2], 16)

            weights(0)
            weights(1)
            context(0, True, [0])
            weights(2)
            context(0, True, [1])
            weights(3)
            context(0, False, [2, 3, 4, 5])
            half = H // 2
            rows8 = lambda w, n: w[n * half * HD:(n + 1) * half * HD, :].rearrange("(h p) d -> p h d", p=HD)
            sp.dma_start(wv_raw[:, 0:half], rows8(wv_t, 0)).then_inc(s_wn, 16)
            context(0, False, [6, 7])
            sp.dma_start(wo_raw[:, 0:half], rows8(wo, 0)).then_inc(s_wn, 16)
            context(0, False, [8, 9])
            sp.wait_ge(s_wused, 2)
            sp.dma_start(wv_raw[:, half:H], rows8(wv_t, 1)).then_inc(s_wn, 16)
            sp.dma_start(wo_raw[:, half:H], rows8(wo, 1)).then_inc(s_wn, 16)
            context(1, False)
            sp.wait_ge(s_z, 2)
            groups = xn_rows[0:DUMP].rearrange("(p r) d -> p r d", p=128)
            sp.dma_start(groups[:, :, 0:D], row[:, 0:1, 0:D].to_broadcast([128, SP_, D])).then_inc(s_zero, 16)
            sp.dma_start(groups[:, :, D + 1:RW], row[:, 0:1, 0:E].to_broadcast([128, SP_, E])).then_inc(s_zero, 16)
            sp.dma_start(xn_rows[0:DUMP, D:D + 1].rearrange("(p r) d -> p (r d)", p=E), empty.bitcast(F32),
                         allow_slow_non_contiguous=True).then_inc(s_zero, 16)
            for n in range(2):
                sp.dma_start(moe_sum[n].rearrange("(p r) d -> p r d", p=SUMP),
                             row[0:SUMP, 0:1, 0:D].to_broadcast([SUMP, (NTOK + CAP) // SUMP, D])).then_inc(s_zero, 16)
            sp.dma_start(gate_w[:], gate_t.rearrange("(c p) e -> p c e", p=128)).then_inc(s_gw, 16)
            for j in range(2):
                sp.dma_start(x1_pair[0:S, j], x[j]).then_inc(s_xin[j], 16)
            with sp.Fori(1, PAIRS) as i:
                for j in range(2):
                    context(2 * i + j, False)
                    sp.wait_ge(s_yst[j], 16 * i)
                    sp.sem_inc(s_lseen, 1)
                    sp.wait_ge(s_row, 2 * i + j - 1)
                    sp.sem_inc(s_lseen, 1)
                    sp.dma_start(x1_pair[0:S, j], x[bass.ds(2 * i + j, 1)].rearrange("o s d -> (o s) d")).then_inc(s_xin[j], 16)

            sp.wait_ge(s_free, fill_number(("q", H // 2 - 1, DC - 1), PAIRS - 1, False, True)[0] + 1)
            sp.dma_start(sgu[:, 0], sg_t.rearrange("(c p) f -> p c f", p=128)).then_inc(s_fw, 16)
            sp.dma_start(sgu[:, 1], su_t.rearrange("(c p) f -> p c f", p=128)).then_inc(s_fw, 16)
            sp.dma_start(shd[:], sd_t.rearrange("(c p) d -> p c d", p=FP)).then_inc(s_fw, 16)
            sp.wait_ge(s_rowst, 16 * (B - 1))
            sp.dma_start(xnt[:, :, 0:(B - 1) * S], xnt_cols[:, :, 0:(B - 1) * S]).then_inc(s_xnt, 16)
            sp.wait_ge(s_yfree, B + 1)

            def expert_weights(e, k, fresh):
                if not fresh:
                    sp.wait_ge(s_wlo, e - NW + 1)
                one = lambda w: w[bass.ds(e, 1)]
                sp.dma_start(wgu[:, k], one(egu_t).rearrange("o p c f -> (o p) c f")).then_inc(s_we[k], 16)
                sp.dma_start(wd[:, k], one(ed_t).rearrange("o p c d -> (o p) c d")).then_inc(s_we[k], 16)

            def expert_rows(e, k, turn, adds, fresh):
                if not fresh:
                    sp.wait_ge(s_add[k % 2], adds)
                src = xn_rows[bass.ds(e * CAP, CAP), :].rearrange("(c p) d -> p c d", p=SP_)
                sp.dma_start(xe[:, k, :, 0:D + 1], src[:, :, 0:D + 1]).then_inc(s_xe[k], 16)
                sp.dma_start(xe[:, k, :, D + 1:D + 1 + UN],
                             xn_rows[bass.ds(e * CAP, CAP), bass.ds(D + 1 + turn * UN, UN)].rearrange("(c p) d -> p c d", p=SP_)).then_inc(s_xe[k], 16)

            for e in range(NW):
                expert_weights(e, e, True)
            for k in range(2):
                sp.wait_ge(s_yst[k], 16 * PAIRS)
            sp.dma_start(x1[0:S], x1_rows.rearrange("b s d -> s b d")).then_inc(s_res, 16)
            for e in range(NW, NW + 2):
                expert_weights(e, e % NW, False)
            sp.wait_ge(s_scat, 16 * B * TOPK)
            for e in range(UN):
                expert_rows(e, e, 0, None, True)
            for e in range(NW + 2, UN):
                expert_weights(e, e % NW, False)
            with sp.Fori(1, E // UN) as i:
                for k in range(UN):
                    expert_weights(i * UN + k, k % NW, False)
                    expert_rows(i * UN + k, k, i, 16 * SC * ((i - 1) * (UN // 2) + k // 2 + 1), False)
            for n in range(2):
                sp.wait_ge(s_add[n], 16 * SC * (E // 2))
                for half in range(2):
                    sp.dma_start(back[0:S, n, half * (B // 2):(half + 1) * (B // 2)],
                                 moe_sum[n][half * (NTOK // 2):(half + 1) * (NTOK // 2), :].rearrange("(b s) d -> s b d", s=S)).then_inc(s_back[n], 16)
            for half in range(2):
                bs = slice(half * (B // 2), (half + 1) * (B // 2))
                sp.wait_ge(s_fin, half + 1)
                sp.dma_start(out[bs].rearrange("b s d -> s b d"), result[0:S, bs]).then_inc(s_out, 16)
            sp.wait_ge(s_out, 32)

        @block.gpsimd
        def _(pool):
            link = [0]

            def chain(ins):
                link[0] += 1
                ins.then_inc(s_pool, 1)
                pool.wait_ge(s_pool, link[0])

            chain(nc.gpsimd.memset(ident[:], 0.0))
            nc.gpsimd.affine_select(out=ident[:], in_=ident[:], compare_op=ALU.not_equal, fill=1.0, base=0,
                                    pattern=[[-1, 128]], channel_multiplier=1).then_inc(s_ident, 1)
            nc.gpsimd.memset(row[:, 0], 0.0).then_inc(s_z, 1)
            nc.gpsimd.iota(empty, [[1, CAP]], base=NTOK, channel_multiplier=0).then_inc(s_z, 1)
            chain(nc.gpsimd.memset(c_hi[:, :, KC - 1, :], 0.0))
            chain(nc.gpsimd.memset(c_lo[:, :, KC - 1, :], 0.0))

            def split(n, j, s_base):
                for k in range(PIECES):
                    loads = 16 * (n * (PIECES // 2 + (k % 2)) + k // 2 + 1) + (16 if k == PIECES - 1 else 0)
                    pool.wait_ge(s_raw[k % 2], loads)
                    pool.sem_inc(s_seen, 1)
                    if k < 4:
                        c, half = k // 2, k % 2
                        cols = slice(half * (KV // 2), (half + 1) * (KV // 2))
                        parts = [(raw[:, k % 2], ct_hi[:, j, c, cols], ct_lo[:, j, c, cols])]
                    else:
                        c = 2 * (k - 4)
                        src = raw[:, k % 2, 0:2 * D].rearrange("p (c d) -> p c d", c=2)
                        if c + 2 < KC:
                            parts = [(src[0:KP], c_hi[0:KP, j, c:c + 2], c_lo[0:KP, j, c:c + 2])]
                        else:
                            parts = [(src[0:r, m], c_hi[0:r, j, c + m], c_lo[0:r, j, c + m]) for m, r in enumerate((KP, KLAST))]
                    for src, hi, lo in parts:
                        last = nc.gpsimd.tensor_scalar(hi, src, F16MAX, -F16MAX, ALU.min, ALU.max)
                    last.then_inc(s_pool, 1)
                    pool.wait_ge(s_pool, s_base + n * PIECES + k + 1)
                    for src, hi, lo in parts:
                        last = nc.gpsimd.tensor_tensor(lo, src, hi, ALU.subtract)
                    last.then_inc(s_split, 1)

            def scale(b, reused):
                if reused:
                    pool.wait_ge(s_scat, 16 * TOPK * (b - 1))
                    pool.sem_inc(s_seen, 1)
                pool.wait_ge(s_moments, b + 1)
                pool.sem_inc(s_seen, 1)
                nc.gpsimd.tensor_tensor(rstd[0:S, 0:1], std[0:S, 0:1], minus_half[0:S], ALU.pow).then_inc(s_scale, 1)

            def store_transposed(b):
                pool.wait_ge(s_rowt, b + 1)
                pool.sem_inc(s_seen, 1)
                pool.dma_start(xnt_cols[:, :, bass.ds(b * S, S)], row_t).then_inc(s_rowst, 16)

            def dispatch(b, j):
                pool.wait_ge(s_slot, b + 1)
                pool.sem_inc(s_seen, 1)
                for k in range(TOPK):
                    nc.gpsimd.indirect_dma_start(xn_rows[:, :], bass.IndirectOffsetOnAxis(ap=scat_u[0:S, j, k:k + 1], axis=0),
                                                 row[0:S, j], None).then_inc(s_scat, 16)

            s_base = link[0]
            split(0, 0, s_base)
            split(1, 1, s_base)
            nc.gpsimd.iota(iota_e[:], [[1, E]], base=0, channel_multiplier=0, allow_small_or_imprecise_dtypes=True).then_inc(s_const, 1)
            nc.gpsimd.iota(dump_row[:], [[1, TOPK]], base=DUMP, channel_multiplier=TOPK,
                           allow_small_or_imprecise_dtypes=True).then_inc(s_const, 1)
            nc.gpsimd.iota(token_f[:], [[1, 1]], base=0, channel_multiplier=1, allow_small_or_imprecise_dtypes=True).then_inc(s_const, 1)
            nc.gpsimd.memset(seen[:], 0.0).then_inc(s_const, 1)
            nc.gpsimd.memset(minus_half[:], -0.5).then_inc(s_const, 1)
            nc.gpsimd.memset(ones[:], 1.0).then_inc(s_const, 1)
            nc.gpsimd.memset(tri[:], 1.0).then_inc(s_pool, 1)
            link[0] += 1
            pool.wait_ge(s_pool, s_base + 2 * PIECES + 1)
            nc.gpsimd.affine_select(out=tri[:], in_=tri[:], compare_op=ALU.is_gt, fill=0.0, base=0,
                                    pattern=[[1, S]], channel_multiplier=-1).then_inc(s_const, 1)
            def batches(i, first):
                for j in range(2):
                    pool.wait_ge(s_yfull, 2 * i + j - 1)
                    scale(2 * i + j - 2, not first)
                    split(2 * i + j, j, s_base + 1)
                    store_transposed(2 * i + j - 2)
                    dispatch(2 * i + j - 2, j)

            batches(1, True)
            with pool.Fori(2, PAIRS) as i:
                batches(i, False)
            scale(B - 2, True)
            store_transposed(B - 2)
            link[0] = s_base + 1 + B * PIECES
            pool.wait_ge(s_fw, 48)
            chain(nc.gpsimd.tensor_scalar(sgu_hi[:], sgu[:], F16MAX, -F16MAX, ALU.min, ALU.max))
            nc.gpsimd.tensor_tensor(sgu_lo[:], sgu[:], sgu_hi[:], ALU.subtract).then_inc(s_shsplit, 1)
            pool.wait_ge(s_xnt, 16)
            toks = slice(0, (B - 1) * S)
            chain(nc.gpsimd.tensor_scalar(xnt_hi[:, :, toks], xnt[:, :, toks], F16MAX, -F16MAX, ALU.min, ALU.max))
            nc.gpsimd.tensor_tensor(xnt_lo[:, :, toks], xnt[:, :, toks], xnt_hi[:, :, toks], ALU.subtract).then_inc(s_shsplit, 1)
            dispatch(B - 2, 0)
            scale(B - 1, True)
            dispatch(B - 1, 1)

            def add_rows(e, k, adds):
                pool.wait_ge(s_eo, e + 1)
                if adds is not None:
                    pool.wait_ge(s_add[k % 2], adds)
                pool.sem_inc(s_seen, 1)
                for h in range(SC):
                    nc.gpsimd.indirect_dma_start(moe_sum[k % 2][:, :], bass.IndirectOffsetOnAxis(ap=xe[:, k, h, D:D + 1].bitcast(U32), axis=0),
                                                 eo[:, k % 2, h, :], None, compute_op=ALU.add).then_inc(s_add[k % 2], 16)

            for e in range(UN):
                add_rows(e, e, None if e < 2 else 16 * SC * (e // 2))
            with pool.Fori(1, E // UN) as i:
                for k in range(UN):
                    add_rows(UN * i + k, k, 16 * SC * (i * (UN // 2) + k // 2))

        @block.scalar
        def _(sc):
            sc.sem_inc(s_exp, 1)
            sc.wait_ge(s_var, 1)
            nc.scalar.activation(std[0:S], rstd[0:S], ACT.Sqrt).then_inc(s_std, 1)
            sc.wait_ge(s_g, 32)
            nc.scalar.activation(gates[:, 2:4], gates[:, 0:2], ACT.Tanh).then_inc(s_tanh, 1)

            def high(n, dst, src, scale=1.0):
                sc.wait_ge(s_full, n + 1)
                nc.scalar.activation(dst, src, ACT.Copy, scale=scale).then_inc(s_hi, 1)

            with sc.Fori(0, H // 4) as i:
                for k in range(4):
                    high(4 * i + k, m_hi[:, bass.ds(4 * i + k, 1)].rearrange("p o c d -> p (o c d)"), setup_bank[:, k, :])
            for u in range(XFILLS):
                high(H + u, xt_hi[:, :, u * 2 * S:(u + 1) * 2 * S], setup_bank[:, u, 0:DC * 2 * S].rearrange("p (c t) -> p c t", c=DC))

            def q_high(n, hp, c, bank):
                high(n, q_hi[:, c, :, hp * 2 * S:(hp + 1) * 2 * S].rearrange("p j (h s) -> p j h s", h=2),
                     stage[:, bank, 0:4 * S].rearrange("p (h j s) -> p j h s", h=2, j=2))

            for hp in range(AHEAD):
                for c in range(DC):
                    q_high(SETUP_FILLS + hp * DC + c, hp, c, (hp * DC + c) % 2)

            def route(b, stage_no, dst=row_t):
                if stage_no == 2:
                    sc.wait_ge(s_rowps, b + 1)
                    if not isinstance(b, int) or 0 < b < B - 1:
                        sc.wait_ge(s_rowst, 16 * b)
                    nc.scalar.activation(dst, row_ps.rearrange("p (c t) -> p c t", c=DC), ACT.Copy).then_inc(s_rowt, 1)
                elif stage_no == 5:
                    sc.wait_ge(s_nmx, b + 1)
                    nc.scalar.activation(ex[0:S], logit_ps[0:S], ACT.Exp, bias=nmx[0:S], scale=1.0, accum_out=esum[0:S]).then_inc(s_ex, 1)

            def pair(i, first, last):
                def fill_hi(f):
                    n, bank = fill_number(f, i, first, last)
                    src = stage[:, bank]
                    if f[0] == "N":
                        high(n, n_hi[:, f[1]].rearrange("p c d -> p (c d)"), src)
                    elif f[0] != "T":
                        q_high(n, f[1], f[2], bank)
                    else:
                        _, t, k = f
                        m = tile_rows(t)
                        off = 128 * (t % TILES - GROUPS[group_of(t)][0])
                        high(n,
                             pt_hi[group_of(t) % 2][0:KP, 4 * k:4 * k + 4, off:off + m],
                             src[0:KP, :].rearrange("p (c q) -> p c q", c=4)[:, :, 0:m])

                for s in range(ALL_STEPS):
                    for f in t_fills(s):
                        fill_hi(f)
                    if s < STEPS:
                        m = tile_rows(s)
                        sc.wait_ge(s_max, i * STEPS + s + 1)
                        nc.scalar.activation(probs[0:m, s % 2, 0:KV], scores[0:m, 0:KV], ACT.Exp,
                                             bias=neg_max[0:m, s % 2:s % 2 + 1], scale=1.0,
                                             accum_out=row_sum[0:m, s % 2:s % 2 + 1]).then_inc(s_exp, 1)
                    for f in q_fills(s) + n_fills(s, first) + ([] if last else ahead_fills(s, False)):
                        fill_hi(f)
                    if s in PV and PV[s][3] == KC:
                        j, g, _, _ = PV[s]
                        w = group_width(g)
                        for c in range(DC):
                            sc.wait_ge(s_accfull, i * 2 * NG * DC + (j * NG + g) * DC + c + 1)
                            nc.scalar.activation(ut_hi[:, c, g * 256:g * 256 + w], acc[:, c, 0:w], ACT.Copy,
                                                 scale=1.0 / PSCALE).then_inc(s_uhi, 1)
                    for f in [] if last else ahead_fills(s, True):
                        fill_hi(f)
                    if s in Y_STEP:
                        j = Y_STEP[s]
                        sc.wait_ge(s_yfree, 2 * i + j + 2)
                        sc.dma_start(x1_rows[bass.ds(2 * i + j, 1)].rearrange("o s d -> (o s) d"), x1_pair[0:S, j]).then_inc(s_yst[j], 16)
                    for j, stage_no in routing_at(s, first):
                        route(2 * i + j, stage_no)

            pair(0, True, False)
            with sc.Fori(1, PAIRS - 1) as i:
                pair(i, False, False)
            pair(PAIRS - 1, False, True)

            def up_high(k, load, used):
                sc.wait_ge(s_we[k], load)
                if used is not None:
                    sc.wait_ge(s_up, used)
                nc.scalar.activation(wgu_hi[:, k], wgu[:, k], ACT.Copy).then_inc(s_guhi, 1)

            def down_high(k, used):
                if used is not None:
                    sc.wait_ge(s_down, used)
                nc.scalar.activation(wd_hi[:, k], wd[:, k], ACT.Copy).then_inc(s_wdhi, 1)

            def rows_high(e, k2):
                sc.wait_ge(s_xt, e + 1)
                nc.scalar.activation(xet_hi[:, k2], stage[:, k2, 0:DC * CAP].rearrange("p (c t) -> p c t", c=DC), ACT.Copy).then_inc(s_xhi, 1)

            def gate(e, k2):
                sc.wait_ge(s_up, e + 1)
                nc.scalar.activation(act[:, k2], ps[0:FP, k2, 0:FC * CAP].rearrange("p (c t) -> p c t", c=FC), ACT.Silu).then_inc(s_act, 1)

            def hidden_high(e, k2):
                sc.wait_ge(s_hid, e + 1)
                nc.scalar.activation(hid_hi[:, k2], hid[:, k2], ACT.Copy).then_inc(s_hhi, 1)

            def expert_out(e, k, adds):
                k2 = k % 2
                sc.wait_ge(s_down, e + 1)
                if adds is not None:
                    sc.wait_ge(s_add[k2], adds)
                for h in range(SC):
                    ins = nc.scalar.activation(eo[:, k2, h], (ps[0:SP_, 2], yps[0:SP_])[k2][:, h * D:(h + 1) * D], ACT.Copy,
                                               scale=xe[:, k, h, D + 1 + k:D + 2 + k])
                ins.then_inc(s_eo, 1)

            def turn(i, first, last):
                for k in range(UN):
                    e, k2 = UN * i + k, k % 2
                    if not (last and k == UN - 1):
                        rows_high(e + 1, (k + 1) % 2)
                    if not (first and k < 2):
                        expert_out(e - 2, (k - 2) % UN, None if first and k < 4 else 16 * SC * (i * (UN // 2) + k // 2 - 1))
                    if not (last and k >= UN - 2):
                        down_high((k + 2) % NW, None if first and k < 2 else e - 1)
                    gate(e, k2)
                    if not (last and k >= UN - 3):
                        up_high((k + 3) % NW, 32 * (i * (UN // NW) + (k + 3) // NW + 1), None if first and k < 1 else e)
                    hidden_high(e, k2)

            last = slice((B - 1) * S, NTOK)
            def shared_gate(u):
                sc.wait_ge(s_shup, u + 1)
                if u >= 3:
                    sc.wait_ge(s_shh, u - 2)
                nc.scalar.activation(sh_act[:, u % 3], ps[0:FP, u % 3, 0:NTOK // 2], ACT.Silu).then_inc(s_shact, 1)

            shared_gate(0)
            shared_gate(1)
            route(B - 1, 2, xnt[:, :, last])
            sc.wait_ge(s_rowt, B)
            nc.scalar.activation(xnt_hi[:, :, last], xnt[:, :, last], ACT.Copy).then_inc(s_lasthi, 1)
            route(B - 1, 5)
            for u in range(2, 2 * FSC):
                shared_gate(u)
                if u >= 6:
                    up_high(u - 6, 32, None)
                    down_high(u - 6, None)
            up_high(2, 32, None)
            rows_high(0, 0)
            turn(0, True, False)
            with sc.Fori(1, E // UN - 1) as i:
                turn(i, False, False)
            turn(E // UN - 1, False, True)
            for e in range(E - 2, E):
                expert_out(e, e % UN, 16 * SC * (E // 2 - 1))

        @block.vector
        def _(dve):
            link = [0]

            def chain(ins):
                link[0] += 1
                ins.then_inc(s_dve, 1)
                dve.wait_ge(s_dve, link[0])

            dve.sem_inc(s_accfree, 1)
            dve.sem_inc(s_yfree, 1)
            dve.wait_ge(s_x, 16)
            for b in range(B):
                ins = nc.vector.bn_stats(stats[0:S, b], x_in[0:S, b])
            chain(ins)
            for b in range(B):
                ins = nc.vector.bn_aggr(mean_var[0:S, b], stats[0:S, b])
            chain(ins)
            nc.vector.tensor_scalar(rstd[0:S], mean_var[0:S, :, 1], EPS, None, ALU.add).then_inc(s_var, 1)

            def low(n, dst, src, hi):
                dve.wait_ge(s_hi, n + 1)
                nc.vector.tensor_tensor(dst, src, hi, ALU.subtract).then_inc(s_free, 1)

            for h in range(H):
                low(h, m_lo[:, h].rearrange("p c d -> p (c d)"), setup_bank[:, h % 4, :], m_hi[:, h].rearrange("p c d -> p (c d)"))
                if h == 0:
                    dve.wait_ge(s_std, 1)
                    chain(nc.vector.reciprocal(rstd[0:S], std[0:S]))
                    chain(nc.vector.tensor_scalar(rstd[0:S], rstd[0:S], QSCALE, None, ALU.mult))
                elif h <= B:
                    nc.vector.tensor_scalar(x_norm[0:S, h - 1], x_in[0:S, h - 1], mean_var[0:S, h - 1, 0:1], rstd[0:S, h - 1:h],
                                            ALU.subtract, ALU.mult).then_inc(s_xnorm, 1)
            for u in range(XFILLS):
                cols = slice(u * 2 * S, (u + 1) * 2 * S)
                low(H + u, xt_lo[:, :, cols], setup_bank[:, u, 0:DC * 2 * S].rearrange("p (c t) -> p c t", c=DC), xt_hi[:, :, cols])
            nc.vector.memset(probs[:, :, KV:KPAD], 0.0).then_inc(s_pads, 1)
            dve.wait_ge(s_tanh, 1)

            def q_low(n, hp, c, bank):
                part = lambda q: q[:, c, :, hp * 2 * S:(hp + 1) * 2 * S].rearrange("p j (h s) -> p j h s", h=2)
                low(n, part(q_lo), stage[:, bank, 0:4 * S].rearrange("p (h j s) -> p j h s", h=2, j=2), part(q_hi))

            for hp in range(AHEAD):
                for c in range(DC):
                    q_low(SETUP_FILLS + hp * DC + c, hp, c, (hp * DC + c) % 2)

            def route(b, stage_no, j):
                done = [links_before(stage_no)]

                def after(semaphore, count):
                    dve.wait_ge(semaphore, count)
                    dve.sem_inc(s_dseen, 1)

                def link(ins):
                    done[0] += 1
                    ins.then_inc(s_route, 1)
                    after(s_route, b * BATCH_LINKS + done[0])

                if stage_no == 0:
                    if isinstance(b, int) and b == 0:
                        dve.wait_ge(s_zero, 80)
                        dve.wait_ge(s_const, 7)
                    after(s_yfree, b + 2)
                    link(nc.vector.bn_stats(stats[0:S, 0], x1_pair[0:S, j]))
                    link(nc.vector.bn_aggr(mean_var[0:S, 0], stats[0:S, 0]))
                    nc.vector.tensor_scalar(std[0:S, 0:1], mean_var[0:S, 0, 1:2], EPS, None, ALU.add).then_inc(s_moments, 1)
                elif stage_no == 1:
                    after(s_scale, b + 1)
                    link(nc.vector.tensor_copy(row[:].bitcast(U32)[0:S, j, D:D + 1], token_f[0:S]))
                    link(nc.vector.tensor_scalar(token_f[0:S], token_f[0:S], float(S), None, ALU.add))
                    nc.vector.tensor_scalar(row[0:S, j, 0:D], x1_pair[0:S, j], mean_var[0:S, 0, 0:1], rstd[0:S, 0:1],
                                            ALU.subtract, ALU.mult).then_inc(s_row, 1)
                elif stage_no == 4:
                    after(s_logit, b + 1)
                    nc.vector.tensor_reduce(nmx[0:S], logit_ps[0:S], AX.X, ALU.max, negate=True).then_inc(s_nmx, 1)
                elif stage_no == 6:
                    after(s_ex, b + 1)
                    link(nc.vector.reciprocal(esum[0:S], esum[0:S]))
                    link(nc.vector.tensor_scalar(ex[0:S], ex[0:S], esum[0:S], None, ALU.mult))
                    link(nc.vector.max(top[0:S], ex[0:S]))
                    link(nc.vector.max_index(topi[0:S], top[0:S], ex[0:S]))
                elif stage_no == 7:
                    link(nc.vector.tensor_reduce(wsum[0:S], top[0:S, 0:TOPK], AX.X, ALU.add))
                    link(nc.vector.tensor_scalar(wsum[0:S], wsum[0:S], 1e-20, None, ALU.add))
                    link(nc.vector.reciprocal(wsum[0:S], wsum[0:S]))
                    link(nc.vector.tensor_copy(topf[0:S], topi[0:S, 0:TOPK]))
                    link(nc.vector.tensor_tensor(hot[0:S], iota_e[0:S].unsqueeze(1).to_broadcast([S, TOPK, E]),
                                                 topf[0:S].unsqueeze(2).to_broadcast([S, TOPK, E]), ALU.is_equal))
                elif stage_no == 8:
                    with nc.allow_low_precision("zeros and ones"):
                        link(nc.vector.tensor_reduce(mask[0:S], hot[0:S].rearrange("p k e -> p e k"), AX.X, ALU.add))
                    link(nc.vector.scalar_tensor_tensor(out=row[0:S, j, D + 1:RW], in0=ex[0:S], scalar=wsum[0:S], in1=mask[0:S],
                                                        op0=ALU.mult, op1=ALU.mult))
                elif stage_no == 10:
                    after(s_pos, b + 1)
                    if not (isinstance(b, int) and b == B - 1):
                        after(s_rowst, 16 * (b + 1))
                    for k0 in range(0, TOPK, KS):
                        k1 = min(k0 + KS, TOPK)
                        link(nc.vector.tensor_tensor(hotpos[0:S, 0:k1 - k0], hot[0:S, k0:k1],
                                                     pos_ps[0:S].unsqueeze(1).to_broadcast([S, k1 - k0, E]), ALU.mult))
                        link(nc.vector.tensor_reduce(pos[0:S, k0:k1], hotpos[0:S, 0:k1 - k0], AX.X, ALU.add))
                    link(nc.vector.tensor_tensor(seen[0:S], seen[0:S], mask[0:S], ALU.add))
                elif stage_no == 11:
                    link(nc.vector.tensor_scalar(over[0:S], pos[0:S], float(CAP), None, ALU.is_ge))
                    link(nc.vector.tensor_scalar(pos[0:S], pos[0:S], float(CAP - 1), None, ALU.min))
                    link(nc.vector.scalar_tensor_tensor(out=slot[0:S], in0=topf[0:S], scalar=float(CAP), in1=pos[0:S], op0=ALU.mult, op1=ALU.add))
                    link(nc.vector.tensor_tensor(scat[0:S], dump_row[0:S], slot[0:S], ALU.subtract))
                    link(nc.vector.tensor_tensor(scat[0:S], scat[0:S], over[0:S], ALU.mult))
                    link(nc.vector.tensor_tensor(scat[0:S], scat[0:S], slot[0:S], ALU.add))
                    link(nc.vector.tensor_scalar(dump_row[0:S], dump_row[0:S], float(S * TOPK), None, ALU.add))
                    nc.vector.tensor_copy(scat_u[0:S, j], scat[0:S]).then_inc(s_slot, 1)
                assert done[0] == links_before(stage_no) + LINKS.get(stage_no, 0)

            def pair(i, first, last):
                def fill_lo(f):
                    n, bank = fill_number(f, i, first, last)
                    src = stage[:, bank]
                    if f[0] == "N":
                        low(n, n_lo[:, f[1]].rearrange("p c d -> p (c d)"), src, n_hi[:, f[1]].rearrange("p c d -> p (c d)"))
                    elif f[0] != "T":
                        q_low(n, f[1], f[2], bank)
                    else:
                        _, t, k = f
                        m = tile_rows(t)
                        off = 128 * (t % TILES - GROUPS[group_of(t)][0])
                        part = lambda p: p[group_of(t) % 2][0:KP, 4 * k:4 * k + 4, off:off + m]
                        low(n, part(pt_lo), src[0:KP, :].rearrange("p (c q) -> p c q", c=4)[:, :, 0:m], part(pt_hi))

                for s in range(ALL_STEPS):
                    fills = t_fills(s)
                    if s < STEPS:
                        m = tile_rows(s)
                        col = slice(s % 2, s % 2 + 1)
                        dve.wait_ge(s_twobanks, i * STEPS + s + 1)
                        nc.vector.tensor_reduce(part_max[0:m, 0:1], scores[0:m, 0:1024], AX.X, ALU.max, negate=True).then_inc(s_part, 1)
                    for f in fills[:2]:
                        fill_lo(f)
                    if s < STEPS:
                        dve.wait_ge(s_scores, i * STEPS + s + 1)
                        nc.vector.tensor_reduce(part_max[0:m, 1:2], scores[0:m, 1024:KV], AX.X, ALU.max, negate=True).then_inc(s_part, 1)
                        dve.wait_ge(s_part, 2 * (i * STEPS + s + 1))
                        nc.vector.tensor_tensor(neg_max[0:m, col], part_max[0:m, 0:1], part_max[0:m, 1:2], ALU.min).then_inc(s_max, 1)
                    for f in fills[2:]:
                        fill_lo(f)
                    if s < STEPS:
                        dve.wait_ge(s_exp, i * STEPS + s + 2)
                        nc.vector.reciprocal(row_inv[0:m, col], row_sum[0:m, col]).then_inc(s_inv, 1)
                        dve.wait_ge(s_inv, i * STEPS + s + 1)
                        nc.vector.tensor_scalar(probs[0:m, s % 2, 0:KV], probs[0:m, s % 2, 0:KV], row_inv[0:m, col], PSCALE,
                                                ALU.mult, ALU.mult).then_inc(s_norm, 1)
                    for f in q_fills(s) + n_fills(s, first) + ([] if last else ahead_fills(s, False)):
                        fill_lo(f)
                    if s in PV and PV[s][3] == KC:
                        j, g, _, _ = PV[s]
                        w = group_width(g)
                        for c in range(DC):
                            dve.wait_ge(s_uhi, i * 2 * NG * DC + (j * NG + g) * DC + c + 1)
                            cols = slice(g * 256, g * 256 + w)
                            nc.vector.scalar_tensor_tensor(out=ut_lo[:, c, cols], in0=acc[:, c, 0:w], scalar=1.0 / PSCALE, in1=ut_hi[:, c, cols],
                                                           op0=ALU.mult, op1=ALU.subtract).then_inc(s_accfree, 1)
                    for f in [] if last else ahead_fills(s, True):
                        fill_lo(f)
                    if s in Y_STEP:
                        j = Y_STEP[s]
                        dve.wait_ge(s_yfull, 2 * i + j + 1)
                        dve.wait_ge(s_xin[j], 16 * (i + 1))
                        nc.vector.scalar_tensor_tensor(out=x1_pair[0:S, j], in0=yps[0:S, 0:D], scalar=gates[0:S, 2:3], in1=x1_pair[0:S, j],
                                                       op0=ALU.mult, op1=ALU.add).then_inc(s_yfree, 1)
                    for j, stage_no in routing_at(s, first):
                        route(2 * i + j, stage_no, j % 2)

            pair(0, True, False)
            with dve.Fori(1, PAIRS - 1) as i:
                pair(i, False, False)
            pair(PAIRS - 1, False, True)

            def up_low(e, k):
                dve.wait_ge(s_guhi, e + 1)
                nc.vector.tensor_tensor(wgu_lo[:, k], wgu[:, k], wgu_hi[:, k], ALU.subtract).then_inc(s_gulo, 1)

            def down_low(e, k):
                dve.wait_ge(s_wdhi, e + 1)
                nc.vector.tensor_tensor(wd_lo[:, k], wd[:, k], wd_hi[:, k], ALU.subtract).then_inc(s_wlo, 1)

            def rows_low(e, k2):
                dve.wait_ge(s_xhi, e + 1)
                nc.vector.tensor_tensor(xet_lo[:, k2], stage[:, k2, 0:DC * CAP].rearrange("p (c t) -> p c t", c=DC), xet_hi[:, k2],
                                        ALU.subtract).then_inc(s_xlo, 1)

            def hidden(e, k2):
                dve.wait_ge(s_act, e + 1)
                nc.vector.tensor_tensor(hid[:, k2], act[:, k2], acc[0:FP, k2, 0:FC * CAP].rearrange("p (c t) -> p c t", c=FC),
                                        ALU.mult).then_inc(s_hid, 1)

            def hidden_low(e, k2):
                dve.wait_ge(s_hhi, e + 1)
                nc.vector.tensor_tensor(hid_lo[:, k2], hid[:, k2], hid_hi[:, k2], ALU.subtract).then_inc(s_hlo, 1)

            def shared_hidden(u):
                half, fc = divmod(u, FSC)
                dve.wait_ge(s_shact, u + 1)
                nc.vector.tensor_tensor(sh_h[:, fc, half * (NTOK // 2):(half + 1) * (NTOK // 2)], sh_act[:, u % 3],
                                        ps[0:FP, SHARED_UP[u % 3], 0:NTOK // 2], ALU.mult).then_inc(s_shh, 1)

            for stage_no in (0, 1, 4):
                route(B - 1, stage_no, 1)
            last_rows = slice((B - 1) * S, NTOK)
            dve.wait_ge(s_lasthi, 1)
            nc.vector.tensor_tensor(xnt_lo[:, :, last_rows], xnt[:, :, last_rows], xnt_hi[:, :, last_rows], ALU.subtract).then_inc(s_shsplit, 1)
            shared_hidden(0)
            shared_hidden(1)
            route(B - 1, 6, 1)
            shared_hidden(2)
            for stage_no in (7, 8):
                route(B - 1, stage_no, 1)
            shared_hidden(3)
            route(B - 1, 10, 1)
            shared_hidden(4)
            shared_hidden(5)
            route(B - 1, 11, 1)

            def shared_out(b):
                dve.wait_ge(s_shdown, b + 1)
                nc.vector.scalar_tensor_tensor(out=x1[0:S, b], in0=ps[0:S, SHARED_DOWN[b % 2], 0:D], scalar=gates[0:S, 3:4],
                                               in1=x1[0:S, b], op0=ALU.mult, op1=ALU.add).then_inc(s_shout, 1)

            dve.wait_ge(s_res, 16)
            for u in range(6, 2 * FSC):
                shared_out(u - 6)
                shared_hidden(u)
                up_low(u - 6, u - 6)
                down_low(u - 6, u - 6)
            for b in range(2, B // 2):
                shared_out(b)
            for b in range(B // 2, B):
                shared_out(b)
                if b == B - 2:
                    rows_low(0, 0)

            def turn(i, first, last):
                for k in range(UN):
                    e, k2 = UN * i + k, k % 2
                    if not (last and k == UN - 1):
                        rows_low(e + 1, (k + 1) % 2)
                    if not (last and k >= UN - 2):
                        up_low(e + 2, (k + 2) % NW)
                    hidden(e, k2)
                    if not (last and k >= UN - 2):
                        down_low(e + 2, (k + 2) % NW)
                    hidden_low(e, k2)

            turn(0, True, False)
            with dve.Fori(1, E // UN - 1) as i:
                turn(i, False, False)
            turn(E // UN - 1, False, True)
            dve.wait_ge(s_back[0], 32)
            chain(nc.vector.scalar_tensor_tensor(out=x1[0:S], in0=back[0:S, 0], scalar=gates[0:S, 3:4], in1=x1[0:S],
                                                 op0=ALU.mult, op1=ALU.add))
            dve.wait_ge(s_back[1], 32)
            for half in range(2):
                bs = slice(half * (B // 2), (half + 1) * (B // 2))
                nc.vector.scalar_tensor_tensor(out=result[0:S, bs], in0=back[0:S, 1, bs], scalar=gates[0:S, 3:4], in1=x1[0:S, bs],
                                               op0=ALU.mult, op1=ALU.add).then_inc(s_fin, 1)

        @block.tensor
        def _(pe):
            def take(n):
                pe.wait_ge(s_free, n - 1)

            def products(dst, pairs, first=True, last=True):
                steps = [(l, r) for lh, ll, rh, rl in pairs for l, r in ((lh, rh), (lh, rl), (ll, rh))]
                for n, (l, r) in enumerate(steps):
                    ins = nc.tensor.matmul(dst, l, r, start=first and n == 0, stop=last and n == len(steps) - 1)
                return ins

            def transposes(src, n, bank, s_done):
                for c in range(DC):
                    for j in range(2):
                        col = (c * 2 + j) * S
                        ins = nc.tensor.transpose(bank[:, col:col + S], src[0:S, 2 * n + j, c * 128:(c + 1) * 128], ident[0:S, 0:S])
                ins.then_inc(s_done, 1)

            pe.wait_ge(s_ident, 1)
            with pe.Fori(0, 6) as i:
                for k in range(5):
                    nc.tensor.transpose(yps[:, 0:128], ident[:], ident[:])
            for i in range(QUADS // 2):
                for k in range(2):
                    pe.wait_ge(s_w[2 * i + k], 32)
                    for h in range(4):
                        if i or k:
                            pe.wait_ge(s_free, (2 * i + k) * 4 + h - 3)
                        first, second = m_factors(2 * i + k)
                        for c in range(DC):
                            ins = nc.tensor.matmul(setup_bank[:, h, c * D:(c + 1) * D], first[:, h, c * 128:(c + 1) * 128], second[:, h, :],
                                                   start=True, stop=True)
                        ins.then_inc(s_full, 1)
                    if i:
                        nc.tensor.transpose(yps[:, 0:128], ident[:], ident[:]).then_inc(s_wused, 1)
            for u in range(XFILLS):
                pe.wait_ge(s_xnorm, 2 * u + 2)
                pe.wait_ge(s_free, H + u - 3)
                transposes(x_norm, u, setup_bank[:, u], s_full)
            pe.wait_ge(s_pads, 1)

            def q_fill(n, bank, pair_no, hp, c):
                take(n)
                for h in range(2):
                    dst = stage[:, bank, h * 2 * S:(h + 1) * 2 * S]
                    cols = slice(c * 128, (c + 1) * 128)
                    toks = bass.ds(pair_no * 2 * S, 2 * S)
                    ins = products(dst, [(m_hi[:, 2 * hp + h, k, cols], m_lo[:, 2 * hp + h, k, cols], xt_hi[:, k, toks], xt_lo[:, k, toks])
                                         for k in range(DC)])
                ins.then_inc(s_full, 1)

            for hp in range(AHEAD):
                for c in range(DC):
                    q_fill(SETUP_FILLS + hp * DC + c, (hp * DC + c) % 2, 0, hp, c)

            def route(b, stage_no, j, rows=row_t):
                if stage_no == 2:
                    if not (isinstance(b, int) and b == 0):
                        pe.wait_ge(s_slot, b)
                    pe.wait_ge(s_row, b + 1)
                    for c in range(DC):
                        ins = nc.tensor.transpose(row_ps[:, c * S:(c + 1) * S], row[0:S, j, c * 128:(c + 1) * 128], ident[0:S, 0:S])
                    ins.then_inc(s_rowps, 1)
                elif stage_no == 3:
                    pe.wait_ge(s_gw, 16)
                    pe.wait_ge(s_rowt, b + 1)
                    for c in range(DC):
                        ins = nc.tensor.matmul(logit_ps[0:S], rows[:, c], gate_w[:, c, :], start=c == 0, stop=c == DC - 1)
                    ins.then_inc(s_logit, 1)
                elif stage_no == 9:
                    pe.wait_ge(s_route, b * BATCH_LINKS + links_before(9))
                    nc.tensor.matmul(pos_ps[0:S], ones[0:S, :], seen[0:S], start=True, stop=False)
                    nc.tensor.matmul(pos_ps[0:S], tri[0:S, :], mask[0:S], start=False, stop=True).then_inc(s_pos, 1)

            def pair(i, first, last):
                def fill(f):
                    kind, hp, c = f
                    n, bank = fill_number(f, i, first, last)
                    if kind == "T":
                        t_fill(n, bank, hp, c)
                    elif kind == "N":
                        pe.wait_ge(s_wn, 64)
                        take(n)
                        for d in range(DC):
                            ins = nc.tensor.matmul(stage[:, bank, d * D:(d + 1) * D], wv_raw[:, hp, d * 128:(d + 1) * 128], wo_raw[:, hp, :],
                                                   start=True, stop=True)
                        ins.then_inc(s_full, 1)
                    else:
                        q_fill(n, bank, i + (kind == "ahead"), hp, c)

                def t_fill(n, bank, t, k):
                    if k == 0:
                        pe.wait_ge(s_norm, i * STEPS + t + 1)
                        if tile_rows(t) < 128:
                            pe.sem_inc(s_pseen, 1)
                    take(n)
                    m = tile_rows(t)
                    if m < 128:
                        pe.sem_inc(s_pseen, 1)
                    for c in range(4):
                        ins = nc.tensor.transpose(stage[0:KP, bank, c * 128:c * 128 + m],
                                                  probs[0:m, t % 2, (4 * k + c) * KP:(4 * k + c + 1) * KP], ident[0:m, 0:m])
                    ins.then_inc(s_full, 1)

                def weighted_sum(j, g, c0, c1):
                    w = group_width(g)
                    if c0 == 0:
                        pe.wait_ge(s_accfree, i * 2 * NG * DC + (j * NG + g) * DC + 1)
                        pe.wait_ge(s_free, fill_number(("T", j * TILES + GROUPS[g][-1], TBANKS - 1), i, first, last)[0] + 1)
                        if g == 0:
                            pe.wait_ge(s_split, (2 * i + j + 1) * PIECES)
                    for c in range(c0, c1):
                        for d in range(DC):
                            cols = slice(d * 128, (d + 1) * 128)
                            ins = products(acc[:, d, 0:w], [(c_hi[0:KP, j, c, cols], c_lo[0:KP, j, c, cols],
                                                             pt_hi[g % 2][0:KP, c, 0:w], pt_lo[g % 2][0:KP, c, 0:w])],
                                           first=c == 0, last=c == KC - 1)
                            if c == KC - 1:
                                ins.then_inc(s_accfull, 1)

                for s in range(ALL_STEPS):
                    fills = t_fills(s)
                    if s < STEPS:
                        j, t = divmod(s, TILES)
                        m = tile_rows(s)
                        if t == 0:
                            pe.wait_ge(s_split, (2 * i + j) * PIECES + 4)
                        hp = min(((s + 1) * 128 - 1) // (2 * S), H // 2 - 1)
                        if s == 0:
                            pe.wait_ge(s_free, FIRST_FILLS if first else LATER_FILLS + i * FILLS)
                        elif AHEAD <= hp and s < TILES:
                            pe.wait_ge(s_free, fill_number(("q", hp, DC - 1), i, first, last)[0] + 1)
                        pe.wait_ge(s_exp, i * STEPS + s + 1)
                        rows = slice(t * 128, t * 128 + m)
                        for n, k0 in enumerate(range(0, KV, 512)):
                            k1 = min(k0 + 512, KV)
                            ins = products(scores[0:m, k0:k1], [(q_hi[:, c, j, rows], q_lo[:, c, j, rows],
                                                                 ct_hi[:, j, c, k0:k1], ct_lo[:, j, c, k0:k1]) for c in range(DC)])
                            if n == 1:
                                ins.then_inc(s_twobanks, 1)
                                for f in fills[:2]:
                                    fill(f)
                        ins.then_inc(s_scores, 1)
                        fills = fills[2:]
                    piece = PV.get(s)
                    if piece:
                        j, g, c0, c1 = piece
                        early = fills + (ahead_fills(s, False) if not last else [])
                        if s < STEPS:
                            weighted_sum(j, g, c0, c0 + 1)
                            for f in early:
                                fill(f)
                            weighted_sum(j, g, c0 + 1, c1)
                            for f in q_fills(s) + n_fills(s, first) + ([] if last else ahead_fills(s, True)):
                                fill(f)
                        else:
                            for k in range(c0, c1, 2):
                                weighted_sum(j, g, k, k + 2)
                                for f in early[:2 if s == STEPS else 1]:
                                    fill(f)
                                early = early[2 if s == STEPS else 1:]
                            assert not early
                            for f in [] if last else ahead_fills(s, True):
                                fill(f)
                    else:
                        for f in fills + q_fills(s) + n_fills(s, first):
                            fill(f)
                    if s in Y_STEP:
                        j = Y_STEP[s]
                        pe.wait_ge(s_accfree, i * 2 * NG * DC + (j + 1) * NG * DC + 1)
                        pe.wait_ge(s_yfree, 2 * i + j + 1)
                        ins = products(yps[0:S, 0:D], [(ut_hi[:, c, h * S:(h + 1) * S], ut_lo[:, c, h * S:(h + 1) * S],
                                                        n_hi[:, h, c, :], n_lo[:, h, c, :]) for h in range(H) for c in range(DC)])
                        ins.then_inc(s_yfull, 1)
                    for j, stage_no in routing_at(s, first):
                        route(2 * i + j, stage_no, j % 2)

            pair(0, True, False)
            with pe.Fori(1, PAIRS - 1) as i:
                pair(i, False, False)
            pair(PAIRS - 1, False, True)

            def shared_up(u):
                half, fc = divmod(u, FSC)
                toks = slice(half * (NTOK // 2), (half + 1) * (NTOK // 2))
                cols = slice(fc * FP, (fc + 1) * FP)
                if u >= 3:
                    pe.wait_ge(s_shh, u - 2)
                for n, bank in enumerate((u % 3, SHARED_UP[u % 3])):
                    ins = products(ps[0:FP, bank, 0:NTOK // 2], [(sgu_hi[:, n, c, cols], sgu_lo[:, n, c, cols], xnt_hi[:, c, toks], xnt_lo[:, c, toks])
                                                                 for c in range(DC)])
                ins.then_inc(s_shup, 1)

            def shared_down(b):
                pe.wait_ge(s_shh, (b // (B // 2) + 1) * FSC)
                if b >= 2:
                    pe.wait_ge(s_shout, b - 1)
                for fc in range(FSC):
                    ins = nc.tensor.matmul(ps[0:S, SHARED_DOWN[b % 2], 0:D], sh_h[:, fc, b * S:(b + 1) * S], shd[:, fc, :],
                                           start=fc == 0, stop=fc == FSC - 1)
                ins.then_inc(s_shdown, 1)

            pe.wait_ge(s_shsplit, 2)
            for u in range(2):
                shared_up(u)
            route(B - 1, 2, 1)
            route(B - 1, 3, 1, xnt[:, :, (B - 1) * S:NTOK])
            shared_up(2)
            shared_up(3)
            pe.wait_ge(s_shsplit, 3)
            shared_up(4)
            route(B - 1, 9, 1)
            for u in range(5, 2 * FSC):
                shared_up(u)
                if u == 5:
                    pe.wait_ge(s_route, (B - 1) * BATCH_LINKS + links_before(11))
                if u == 6:
                    pe.wait_ge(s_shh, 6)
                shared_down(u - 5)
            shared_down(3)

            def rows_in(e, k, guard, loads):
                pe.wait_ge(s_xe[k], loads)
                if guard:
                    pe.wait_ge(s_xlo, e - 1)
                for c in range(DC):
                    for h in range(SC):
                        ins = nc.tensor.transpose(stage[:, k % 2, c * CAP + h * SP_:c * CAP + (h + 1) * SP_],
                                                  xe[:, k, h, c * 128:(c + 1) * 128], ident[0:SP_, 0:SP_])
                ins.then_inc(s_xt, 1)

            def up(e, k, guard):
                pe.wait_ge(s_wlo, e + 1)
                pe.wait_ge(s_xlo, e + 1)
                if guard:
                    pe.wait_ge(s_hid, e - 1)
                k2 = k % 2
                for which, dst in enumerate((ps[0:FP, k2], acc[0:FP, k2])):
                    for fc in range(FC):
                        cols = slice(which * F + fc * FP, which * F + (fc + 1) * FP)
                        ins = products(dst[:, fc * CAP:(fc + 1) * CAP], [(wgu_hi[:, k, c, cols], wgu_lo[:, k, c, cols],
                                                                          xet_hi[:, k2, c], xet_lo[:, k2, c]) for c in range(DC)])
                ins.then_inc(s_up, 1)

            def down(e, k, guard):
                pe.wait_ge(s_hlo, e + 1)
                if guard:
                    pe.wait_ge(s_eo, e - 1)
                k2 = k % 2
                dst = (ps[0:SP_, 2], yps[0:SP_])[k2]
                for h in range(SC):
                    slots = slice(h * SP_, (h + 1) * SP_)
                    ins = products(dst[:, h * D:(h + 1) * D], [(hid_hi[:, k2, fc, slots], hid_lo[:, k2, fc, slots],
                                                                wd_hi[:, k, fc], wd_lo[:, k, fc]) for fc in range(FC)])
                ins.then_inc(s_down, 1)

            def turn(i, first, last):
                for k in range(UN):
                    e = UN * i + k
                    if not (last and k == UN - 1):
                        rows_in(e + 1, (k + 1) % UN, not (first and k == 0), 32 * (i + 1 + (k + 1) // UN))
                    up(e, k % NW, not (first and k < 2))
                    if not (first and k == 0):
                        down(e - 1, (k - 1) % NW, not (first and k < 3))

            for b in range(B // 2, B):
                shared_down(b)
                if b == B - 2:
                    rows_in(0, 0, False, 32)
            pe.wait_ge(s_shout, B)
            turn(0, True, False)
            with pe.Fori(1, E // UN - 1) as i:
                turn(i, False, False)
            turn(E // UN - 1, False, True)
            down(E - 1, NW - 1, True)


def kernel(**inputs):
    import numpy as _np
    import concourse.bacc as _bacc
    from concourse import mybir as _mybir
    from concourse.bass_utils import run_bass_kernel_spmd as _run

    a = {k: _np.asarray(v) for k, v in inputs.items()}

    def chunks(w, p):
        e, r, c = w.shape
        return w.reshape(e, r // p, p, c).transpose(0, 2, 1, 3)

    ins = {
        "x": a["x"],
        "ctx_rows": a["ctx_2048"],
        "ctx_cols": a["ctx_2048"].transpose(0, 2, 1),
        "wq_t": a["L0_xattn_Wq"].T,
        "wk_t": a["L0_xattn_Wk"].T,
        "wv_t": a["L0_xattn_Wv"].T,
        "wo": a["L0_xattn_Wo"],
        "g_xattn": a["g_xattn"],
        "g_ffn": a["g_ffn"],
        "gate_t": a["L0_ffn_gate_w"].T,
        "egu_t": chunks(_np.concatenate([a["L0_ffn_w_gate"], a["L0_ffn_w_up"]], axis=1).transpose(0, 2, 1), 128),
        "ed_t": chunks(a["L0_ffn_w_down"].transpose(0, 2, 1), 88),
        "sg_t": a["L0_ffn_sh_gate"].T,
        "su_t": a["L0_ffn_sh_up"].T,
        "sd_t": a["L0_ffn_sh_down"].T,
    }
    nc = _bacc.Bacc("TRN2", target_bir_lowering=False, num_devices=1)
    arrays, args = {}, []
    for name, v in ins.items():
        v = _np.ascontiguousarray(v)
        arrays[f"in_{name}"] = v
        args.append(nc.dram_tensor(f"in_{name}", v.shape, _mybir.dt.from_np(v.dtype), kind="ExternalInput").ap())
    args.append(nc.dram_tensor("out_y", (8, 100, 256), _mybir.dt.float32, kind="ExternalOutput").ap())
    gated_cross_attention_moe(nc, *args)
    r = _run(nc, [arrays], core_ids=[0])
    return r.results[0]["out_y"]
```
